# Optimizing a Trainium2 kernel written in Bass

```python
import numpy as np
import jax
import jax.numpy as jnp

def _softmax(x, axis=-1):
    return jax.nn.softmax(x, axis=axis)
def _gelu(x):
    return jax.nn.gelu(x, approximate=True)
def _silu(x):
    return jax.nn.silu(x)
def _sigmoid(x):
    return jax.nn.sigmoid(x)
def _layernorm(x, axis=-1, eps=1e-5):
    m = jnp.mean(x, axis=axis, keepdims=True)
    v = jnp.var(x, axis=axis, keepdims=True)
    return (x - m) / jnp.sqrt(v + eps)
def _scatter_add(tgt, idx, src, axis=0):
    return tgt.at[idx].add(src)
def _segment_sum(src, seg, n):
    return jax.ops.segment_sum(src, seg, n)

kernel_name = 'mk_conv_preact_d2_conv_nchw192_b24503'

def setup_inputs(seed: int = 0):
    np.random.seed(seed)
    _w = jnp.asarray
    def _rec_inputs():
        import jax
        import jax.numpy as jnp
        _gk = jax.random.key(seed)
        x = -0.0001538 + 1 * jax.random.normal(jax.random.fold_in(_gk, 1), (8, 192, 64, 64), jnp.float32)
        return x
    x = _rec_inputs()
    def _L0_conv_setup():
        import jax, jax.numpy as jnp
        import numpy as np
        B, C, H, W = (8, 192, 64, 64)
        RED = 8
        CR = C // RED

        def prelu(x, a):
            return jnp.where(x >= 0, x, a * x)

        def conv1x1(x, w, b):
            return jnp.einsum('bchw,oc->bohw', x, w) + b[None, :, None, None]
        key = jax.random.key(seed)
        ks = jax.random.split(key, 7)
        scale1 = 1.0 / np.sqrt(C)
        return {'x': jax.random.normal(ks[0], (B, C, H, W), dtype=jnp.float32), 'w1': jax.random.uniform(ks[1], (CR, C), jnp.float32, -scale1, scale1), 'b1': jnp.zeros((CR,), jnp.float32), 'a1': jnp.full((1,), 0.25, jnp.float32), 'w2': jax.random.uniform(ks[2], (CR, C), jnp.float32, -scale1, scale1), 'b2': jnp.zeros((CR,), jnp.float32), 'a2': jnp.full((1,), 0.25, jnp.float32), 'wa': jax.random.uniform(ks[3], (C, C), jnp.float32, -scale1, scale1), 'ba': jnp.zeros((C,), jnp.float32), 'aa': jnp.full((1,), 0.25, jnp.float32)}
    _L0_conv_all = _L0_conv_setup()
    _L0_conv_in = {k: v for k, v in _L0_conv_all.items() if k in ('w1', 'b1', 'a1', 'w2', 'b2', 'a2', 'wa', 'ba', 'aa', )}
    del _L0_conv_all

    def _L1_conv_setup():
        import jax, jax.numpy as jnp
        import numpy as np
        CHANNEL = 192
        FILTERS = (1, 3, 3, 3, 1)
        N_LAYERS = 4
        INIT_SCALE = 10.0

        def _logits_cumulative(logits, ms, bs, fs):
            for i in range(N_LAYERS):
                logits = jnp.einsum('cij,cjn->cin', jax.nn.softplus(ms[i]), logits) + bs[i]
                if i < N_LAYERS - 1:
                    logits = logits + jnp.tanh(fs[i]) * jnp.tanh(logits)
            return logits
        key = jax.random.key(seed)
        keys = jax.random.split(key, 16)
        x = jax.random.normal(keys[0], (16, CHANNEL, 64, 64), dtype=jnp.float32)
        scale = INIT_SCALE ** (1.0 / N_LAYERS)
        inp = {'x': x}
        for i in range(N_LAYERS):
            f_in, f_out = (FILTERS[i], FILTERS[i + 1])
            init = float(np.log(np.expm1(1.0 / scale / f_out)))
            inp[f'm{i}'] = jnp.full((CHANNEL, f_out, f_in), init, dtype=jnp.float32)
            inp[f'b{i}'] = jax.random.uniform(keys[1 + i], (CHANNEL, f_out, 1), minval=-0.5, maxval=0.5, dtype=jnp.float32)
            if i < N_LAYERS - 1:
                inp[f'f{i}'] = jnp.zeros((CHANNEL, f_out, 1), dtype=jnp.float32)
        return inp
    _L1_conv_all = _L1_conv_setup()
    _L1_conv_in = {k: v for k, v in _L1_conv_all.items() if k in ('m0', 'm1', 'm2', 'm3', 'b0', 'b1', 'b2', 'b3', 'f0', 'f1', 'f2', )}
    del _L1_conv_all

    return {
        "x": x,
        "L0_conv_w1": _L0_conv_in["w1"],
        "L0_conv_b1": _L0_conv_in["b1"],
        "L0_conv_a1": _L0_conv_in["a1"],
        "L0_conv_w2": _L0_conv_in["w2"],
        "L0_conv_b2": _L0_conv_in["b2"],
        "L0_conv_a2": _L0_conv_in["a2"],
        "L0_conv_wa": _L0_conv_in["wa"],
        "L0_conv_ba": _L0_conv_in["ba"],
        "L0_conv_aa": _L0_conv_in["aa"],
        "L1_conv_m0": _L1_conv_in["m0"],
        "L1_conv_m1": _L1_conv_in["m1"],
        "L1_conv_m2": _L1_conv_in["m2"],
        "L1_conv_m3": _L1_conv_in["m3"],
        "L1_conv_b0": _L1_conv_in["b0"],
        "L1_conv_b1": _L1_conv_in["b1"],
        "L1_conv_b2": _L1_conv_in["b2"],
        "L1_conv_b3": _L1_conv_in["b3"],
        "L1_conv_f0": _L1_conv_in["f0"],
        "L1_conv_f1": _L1_conv_in["f1"],
        "L1_conv_f2": _L1_conv_in["f2"],
    }

def reference(x, L0_conv_w1, L0_conv_b1, L0_conv_a1, L0_conv_w2, L0_conv_b2, L0_conv_a2, L0_conv_wa, L0_conv_ba, L0_conv_aa, L1_conv_m0, L1_conv_m1, L1_conv_m2, L1_conv_m3, L1_conv_b0, L1_conv_b1, L1_conv_b2, L1_conv_b3, L1_conv_f0, L1_conv_f1, L1_conv_f2):
    import jax
    import jax.numpy as jnp
    def _L0_conv_ref(x, w1, b1, a1, w2, b2, a2, wa, ba, aa):
        import jax, jax.numpy as jnp
        import numpy as np
        B, C, H, W = (8, 192, 64, 64)
        RED = 8
        CR = C // RED

        def prelu(x, a):
            return jnp.where(x >= 0, x, a * x)

        def conv1x1(x, w, b):
            return jnp.einsum('bchw,oc->bohw', x, w) + b[None, :, None, None]
        b, c, h, w = x.shape
        hw = h * w
        q = prelu(conv1x1(x, w1, b1), a1)
        k = prelu(conv1x1(x, w2, b2), a2)
        v = prelu(conv1x1(x, wa, ba), aa)
        q = q.reshape(b, -1, hw).transpose(0, 2, 1)
        k = k.reshape(b, -1, hw)
        score = jax.nn.softmax(jnp.einsum('bnc,bcm->bnm', q, k), axis=2)
        v = v.reshape(b, c, hw).transpose(0, 2, 1)
        out = jnp.einsum('bnm,bmc->bnc', score, v)
        return out.transpose(0, 2, 1).reshape(b, c, h, w)

    def _L1_conv_ref(x, m0, m1, m2, m3, b0, b1, b2, b3, f0, f1, f2):
        import jax, jax.numpy as jnp
        import numpy as np
        CHANNEL = 192
        FILTERS = (1, 3, 3, 3, 1)
        N_LAYERS = 4
        INIT_SCALE = 10.0

        def _logits_cumulative(logits, ms, bs, fs):
            for i in range(N_LAYERS):
                logits = jnp.einsum('cij,cjn->cin', jax.nn.softplus(ms[i]), logits) + bs[i]
                if i < N_LAYERS - 1:
                    logits = logits + jnp.tanh(fs[i]) * jnp.tanh(logits)
            return logits
        ms = (m0, m1, m2, m3)
        bs = (b0, b1, b2, b3)
        fs = (f0, f1, f2)
        B, C, H, W = x.shape
        xr = jnp.transpose(x, (1, 0, 2, 3)).reshape(C, 1, -1)
        lower = _logits_cumulative(xr - 0.5, ms, bs, fs)
        upper = _logits_cumulative(xr + 0.5, ms, bs, fs)
        sign = jax.lax.stop_gradient(-jnp.sign(lower + upper))
        likelihood = jnp.abs(jax.nn.sigmoid(sign * upper) - jax.nn.sigmoid(sign * lower))
        likelihood = jnp.maximum(likelihood, 1e-06)
        likelihood = likelihood.reshape(C, B, H, W)
        return jnp.transpose(likelihood, (1, 0, 2, 3))

    def _gn(v, G=32, eps=1e-5):
        B_, C_, H_, W_ = v.shape
        g = v.reshape(B_, G, C_ // G, H_, W_)
        m = jnp.mean(g, axis=(2, 3, 4), keepdims=True)
        s = jnp.var(g, axis=(2, 3, 4), keepdims=True)
        return ((g - m) / jnp.sqrt(s + eps)).reshape(v.shape)

    def _ln_c(v, eps=1e-6):
        m = jnp.mean(v, axis=1, keepdims=True)
        s = jnp.var(v, axis=1, keepdims=True)
        return (v - m) / jnp.sqrt(s + eps)

    def _ln_t(v, eps=1e-5):
        m = jnp.mean(v, axis=-1, keepdims=True)
        s = jnp.var(v, axis=-1, keepdims=True)
        return (v - m) / jnp.sqrt(s + eps)

    def _to_tokens(v):
        B_, C_, H_, W_ = v.shape
        return v.reshape(B_, C_, H_ * W_).transpose(0, 2, 1)
    def _from_tokens(t, like):
        B_, C_, H_, W_ = like.shape
        return t.transpose(0, 2, 1).reshape(B_, C_, H_, W_)

    x = x + _L0_conv_ref(_gn(x), L0_conv_w1, L0_conv_b1, L0_conv_a1, L0_conv_w2, L0_conv_b2, L0_conv_a2, L0_conv_wa, L0_conv_ba, L0_conv_aa)
    x = x + _L1_conv_ref(_gn(x), L1_conv_m0, L1_conv_m1, L1_conv_m2, L1_conv_m3, L1_conv_b0, L1_conv_b1, L1_conv_b2, L1_conv_b3, L1_conv_f0, L1_conv_f1, L1_conv_f2)
    return x


_drawn_inputs = setup_inputs


def setup_inputs(seed=0):
    import zlib

    import numpy as np

    out = dict(_drawn_inputs(seed))
    spreads = {'L0_conv_b1': (0.0, 2.0),
     'L0_conv_b2': (0.0, 2.0),
     'L0_conv_ba': (0.0, 0.1),
     'L1_conv_m0': (-1.5790714025497437, 0.6),
     'L1_conv_m1': (-1.5790714025497437, 0.6),
     'L1_conv_m2': (-1.5790714025497437, 0.6),
     'L1_conv_m3': (-0.2813340127468109, 0.6),
     'L1_conv_f0': (0.0, 2.0),
     'L1_conv_f1': (0.0, 2.0),
     'L1_conv_f2': (0.0, 2.0)}
    factors = {'L1_conv_b0': 200.0, 'L1_conv_b1': 176.301, 'L1_conv_b2': 200.0, 'L1_conv_b3': 196.094}
    for name, (base, spread) in spreads.items():
        noise = np.random.default_rng([zlib.crc32(name.encode()), seed]).standard_normal(out[name].shape)
        drawn = base * np.exp(spread * noise) if base else spread * noise
        out[name] = jnp.asarray(drawn.astype(out[name].dtype))
    for name, factor in factors.items():
        out[name] = (out[name] * factor).astype(out[name].dtype)
    return out
```

```python
from contextlib import ExitStack

import concourse.bass as bass
from concourse import mybir

ALU = mybir.AluOpType
ACT = mybir.ActivationFunctionType
F32 = mybir.dt.float32
F16 = mybir.dt.float16
AX_X = mybir.AxisListType.X

B, C, HW = 8, 192, 64 * 64
CR = C // 8
P = 128
HALF = C // 2
N = 512
BLOCKS = HW // N
NT = N // P
MT = HW // P
PAIRS = MT // 2
MAXES = NT * BLOCKS
SUB = 32
VW = C + 2
EPS = 1e-5
LN2 = 0.6931471805599453
ESHIFT = 14 * LN2
BIG = 4096.0
PER_STEP = 3

COL_BQ, COL_BK, COL_A1, COL_A2, COL_AA, COL_MQ, COL_MK = range(7)
NCOLS = 7
CONST_DMAS = 10

G = 32
GROUPS = C // G
HID = 3
HR = HID * G
CHUNKS = 4
UN = CHUNKS * N
WCOLS = HR + HR + G
SC_SP0, SC_BL, SC_BU, SC_C1, SC_C2, SC_T1, SC_T2, SC_C3 = range(WCOLS, WCOLS + 8)
WROW = WCOLS + 8
UNITS = 2 * GROUPS
SLOTS = UNITS * CHUNKS

M0, M1, M2, M3 = 0, 3, 12, 21
M1C, M2C, M3C = 24, 27, 30
M0R, M1R, M2R = 31, 32, 35
NM = 38
F0O, F1O, F2O = 0, 1, 2
NF = 3
B0, B1, B2, B3, B0O, B1O, B2O = 0, 3, 6, 9, 10, 11, 12
NB = 13

SETUP_STEPS = 9 + 3 * 6 + 9 * 6 + 7
STAT_STEPS = 11
MAX_STEPS = 6


def program(nc, x, wqk, wv, cols, g6, eye, diag, mraw, fraw, braw, out, x2_dram, xn_dram):
    x_rows = x.rearrange("b c h w -> (b c) (h w)")
    out_rows = out.rearrange("b c h w -> (b c) (h w)")
    with ExitStack() as ctx:
        def sb(name, shape, dt=F32):
            return ctx.enter_context(nc.sbuf_tensor(name, shape, dt))

        def sem(name):
            return ctx.enter_context(nc.semaphore(name))

        x_sb = sb("x_sb", [HALF, 2, HW])
        xn = sb("xn", [HALF + 1, 2, HW])
        wqk_sb = sb("wqk_sb", [HALF, 2, 2, P])
        wv_sb = sb("wv_sb", [HALF + 1, 2, C])
        cols_sb = sb("cols_sb", [P, NCOLS])
        ncols = sb("ncols", [P, NCOLS])
        g6_sb = sb("g6_sb", [HALF, HALF])
        eye_sb = sb("eye_sb", [P, P])
        eye16 = sb("eye16", [P, P], F16)
        diag_sb = sb("diag_sb", [P, G])
        stats = sb("stats", [HALF, 2, BLOCKS, 6])
        mv = sb("mv", [HALF, 2, 2])
        gmean = sb("gmean", [HALF, 2])
        gvar = sb("gvar", [HALF, 2])
        gstd = sb("gstd", [HALF, 2])
        rstd = sb("rstd", [HALF, 2])
        tmp_a = sb("tmp_a", [HALF, 2])
        tmp_b = sb("tmp_b", [HALF, 2])
        mxp = sb("mxp", [P, NT, BLOCKS])
        mx = sb("mx", [P, NT])
        negm = sb("negm", [P, NT])
        rest = sb("rest", [P, NT])
        mparts = sb("mparts", [P, 3, NT], F16)
        mrows = sb("mrows", [3 * NT, P], F16)
        rden = sb("rden", [P, NT])
        w_all = sb("w_all", [P, GROUPS, WROW])
        msp = sb("msp", [P, GROUPS, NM])
        fth = sb("fth", [P, GROUPS, NF])
        bra = sb("bra", [P, GROUPS, NB])
        sp_abs = sb("sp_abs", [P, GROUPS, NM])
        sp_e = sb("sp_e", [P, GROUPS, NM])
        sp_u = sb("sp_u", [P, GROUPS, NM])
        sp_l = sb("sp_l", [P, GROUPS, NM])
        coef = sb("coef", [P, GROUPS, HID])
        c1_all = sb("c1_all", [P, GROUPS, HID])
        c2_all = sb("c2_all", [P, GROUPS, HID])
        prod = sb("prod", [P, GROUPS])

        arena = sb("arena", [P, 30720])
        place = [0]

        def take(words):
            place[0] += words
            return arena[:, place[0] - words:place[0]]

        kst = take(HW // 2).bitcast(F16)
        qst = take(HW // 2).bitcast(F16)
        v_sb = take(MT * (VW + C) // 2).bitcast(F16).rearrange("p (m n) -> p m n", m=MT)
        e_hi = take(4 * N).bitcast(F16).rearrange("p (s n) -> p s n", s=4)
        e_lo = take(4 * N).bitcast(F16).rearrange("p (s n) -> p s n", s=4)
        e_32 = take(2 * 2 * N).rearrange("p (s n) -> p s n", s=2)
        o_sb = take(2 * NT * C).rearrange("p (s t n) -> p s t n", s=2, t=NT)
        p_pos = take(2 * N).rearrange("p (s n) -> p s n", s=2)
        p_neg = take(2 * N).rearrange("p (s n) -> p s n", s=2)
        p_val = take(2 * N).rearrange("p (s n) -> p s n", s=2)
        p_hi = take(N).bitcast(F16).rearrange("p (s n) -> p s n", s=2)
        place[0] = 0
        x4 = take(2 * UN).rearrange("p (s n) -> p s n", s=2)
        t0 = take(2 * 2 * UN).rearrange("p (s d n) -> p s d n", s=2, d=2)
        t1 = take(2 * 2 * N).rearrange("p (s d n) -> p s d n", s=2, d=2)
        t2 = take(2 * 2 * N).rearrange("p (s d n) -> p s d n", s=2, d=2)
        h1 = take(2 * 2 * N).rearrange("p (s d n) -> p s d n", s=2, d=2)
        h2 = take(4 * 2 * N).rearrange("p (s d n) -> p s d n", s=4, d=2)
        lu = take(2 * 2 * N).rearrange("p (s d n) -> p s d n", s=2, d=2)
        lu_sum = take(N)
        lu_sign = take(N)
        signed = take(2 * N).rearrange("p (d n) -> p d n", d=2)
        sig = take(2 * N).rearrange("p (d n) -> p d n", d=2)
        dif = take(N)
        size = take(N)
        res = take(2 * N).rearrange("p (s n) -> p s n", s=2)
        x2t = take(2 * N).rearrange("p (s n) -> p s n", s=2)

        ps = ctx.enter_context(nc.psum_tensor("ps", [P, 8, N], F32))

        def own_banks(g):
            return 4 + 2 * (g % 2)

        consts_in = sem("consts_in")
        set_step = sem("set_step")
        set_act = sem("set_act")
        set_gp = sem("set_gp")
        ones_col = sem("ones_col")
        x_in = sem("x_in")
        x_stat = sem("x_stat")
        stat_step = sem("stat_step")
        stat_mm = sem("stat_mm")
        stat_std = sem("stat_std")
        xn_ready = sem("xn_ready")
        proj_mm = sem("proj_mm")
        proj_act = sem("proj_act")
        proj_val = sem("proj_val")
        proj_hi = sem("proj_hi")
        proj_done = sem("proj_done")
        max_mm = sem("max_mm")
        max_red = sem("max_red")
        max_step = sem("max_step")
        max_turn = sem("max_turn")
        max_rows = sem("max_rows")
        max_in = sem("max_in")
        scored = sem("scored")
        full_ready = sem("full_ready")
        lo_ready = sem("lo_ready")
        summed = sem("summed")
        den_ready = sem("den_ready")
        out_norm = sem("out_norm")
        out_turn = sem("out_turn")
        x2_ready = sem("x2_ready")
        x2_stat = sem("x2_stat")
        x2_out = sem("x2_out")
        xn_out = [sem(f"xn_out{h}") for h in range(2)]
        x4_in = [sem(f"x4_in{s}") for s in range(2)]
        x2t_in = [sem(f"x2t_in{s}") for s in range(2)]
        x_side = sem("x_side")
        t0_ready = sem("t0_ready")
        h1_mm = sem("h1_mm")
        t1_ready = sem("t1_ready")
        h1_ready = sem("h1_ready")
        h2_mm = sem("h2_mm")
        t2_ready = sem("t2_ready")
        h2_ready = sem("h2_ready")
        h3_mm = sem("h3_mm")
        lu_ready = sem("lu_ready")
        sum_ready = sem("sum_ready")
        sign_ready = sem("sign_ready")
        signed_ready = sem("signed_ready")
        sig_ready = sem("sig_ready")
        dif_ready = sem("dif_ready")
        size_ready = sem("size_ready")
        res_ready = sem("res_ready")
        stored = [sem(f"stored{s}") for s in range(2)]

        HALF_UNITS = UNITS // 2 * 16

        def settle(eng):
            eng.wait_ge(consts_in, CONST_DMAS * 16)
        block = ctx.enter_context(nc.Block())

        @block.sync
        def _(sp):
            for h in range(2):
                sp.dma_start(x_sb[:, h, :], x_rows[h * HALF:(h + 1) * HALF, :]).then_inc(x_in, 16)
            for dst, src in ((cols_sb[:, :], cols), (g6_sb[:, :], g6),
                             (wqk_sb[:, :, :, :], wqk.rearrange("(h p) k n -> p h k n", h=2)),
                             (wv_sb[0:HALF, :, :], wv[0:C, :].rearrange("(h p) n -> p h n", h=2)),
                             (wv_sb[HALF:HALF + 1, 1, :], wv[C:C + 1, :]),
                             (eye_sb[:, :], eye), (diag_sb[:, :], diag), (msp[:, :, :], mraw),
                             (fth[:, :, :], fraw), (bra[:, :, :], braw)):
                sp.dma_start(dst, src).then_inc(consts_in, 16)

            def image(b, row, last):
                sp.wait_ge(max_rows, b * BLOCKS + 1)
                sp.dma_start(qst[CR:CR + 3, 0:N].rearrange("r (t n) -> r t n", t=NT),
                             mrows[:, :]).then_inc(max_in, 16)
                with sp.Fori(1, BLOCKS) as j:
                    col = sp.compute_val(j * N)
                    sp.wait_ge(max_rows, b * BLOCKS + j + 1)
                    sp.dma_start(qst[CR:CR + 3, bass.ds(col, N)].rearrange("r (t n) -> r t n", t=NT),
                                 mrows[:, :]).then_inc(max_in, 16)
                for h in range(2):
                    sp.wait_ge(x2_ready, b * 2 * BLOCKS + 2 * BLOCKS - 1 + h)
                    sp.dma_start(x2_dram[bass.ds(row + h * HALF, HALF), :], x_sb[:, h, :]).then_inc(x2_out, 16)
                for h in range(2):
                    sp.wait_ge(xn_ready, b * 4 + 3 + h)
                    sp.dma_start(xn_dram[bass.ds(row + h * HALF, HALF), :],
                                 xn[0:HALF, h, :]).then_inc(xn_out[h], 16)
                sp.wait_ge(x2_out, b * 32 + 32)
                for u in range(UNITS):
                    s = u % 2
                    channel = sp.compute_val(row + (u // 2) * G)
                    norm_out = sp.compute_val(b * 16 + 16)
                    tanh_read = sp.compute_val(b * SLOTS + max(u - 1, 0) * CHUNKS)
                    side_read = sp.compute_val(b * UNITS + max(u - 1, 0))
                    if u % (UNITS // 2) == 0:
                        settle(sp)
                        sp.wait_ge(xn_out[u // (UNITS // 2)], norm_out)
                    if u >= 2:
                        settle(sp)
                        sp.wait_ge(t0_ready, tanh_read)
                        sp.wait_ge(x_side, side_read)
                    for k in range(4):
                        sp.dma_start(x4[k * G:(k + 1) * G, s, :],
                                     xn_dram[bass.ds(channel, G), s * UN:(s + 1) * UN]).then_inc(x4_in[s], 16)
                    if u >= 2:
                        store(b, row, u - 2)
                    sp.dma_start(x2t[:, s, :],
                                 x2_dram[bass.ds(channel, G), s * UN:(s + 1) * UN]
                                 .rearrange("c (k n) -> k c n", k=CHUNKS)).then_inc(x2t_in[s], 16)
                    if u == 1 and not last:
                        for h in range(2):
                            sp.dma_start(x_sb[:, h, :],
                                         x_rows[bass.ds(row + (2 + h) * HALF, HALF), :]).then_inc(x_in, 16)
                store(b, row, UNITS - 2)
                store(b, row, UNITS - 1)

            def store(b, row, u):
                sp.wait_ge(res_ready, b * UNITS + u + 1)
                sp.dma_start(out_rows[bass.ds(row + (u // 2) * G, G), (u % 2) * UN:(u % 2 + 1) * UN]
                             .rearrange("c (k n) -> k c n", k=CHUNKS), res[:, u % 2, :]).then_inc(stored[u % 2], 16)

            with sp.Fori(0, B - 1) as b:
                image(b, sp.compute_val(b * C), False)
            image(B - 1, (B - 1) * C, True)
            for s in range(2):
                sp.wait_ge(stored[s], B * HALF_UNITS)

        @block.gpsimd
        def _(pool):
            pool.memset(xn[HALF:HALF + 1, :, :], 1.0).then_inc(set_gp, 1)
            pool.wait_ge(set_gp, 1)
            pool.wait_ge(set_step, SETUP_STEPS)
            for g in range(GROUPS):
                for i in range(HID):
                    pool.tensor_scalar(w_all[:, g, i * G:(i + 1) * G], diag_sb[:, :], coef[:, g, i:i + 1], None,
                                       ALU.mult)
                    pool.tensor_scalar(w_all[0:HR, g, HR + i * G:HR + (i + 1) * G], diag_sb[0:HR, :],
                                       msp[0:HR, g, M2C + i:M2C + i + 1], None, ALU.mult)
                ins = pool.tensor_scalar(w_all[0:HR, g, 2 * HR:WCOLS], diag_sb[0:HR, :],
                                         msp[0:HR, g, M3C:M3C + 1], None, ALU.mult)
            ins.then_inc(set_gp, 1)
            with pool.Fori(0, B) as b:
                results, stores = pool.compute_val(b * UNITS), pool.compute_val(b * HALF_UNITS)
                settle(pool)
                pool.wait_ge(res_ready, results)
                for s in range(2):
                    pool.wait_ge(stored[s], stores)
                pool.memset(v_sb[:, :, C:VW], 1.0).then_inc(ones_col, 1)

                def sides(u):
                    s = u % 2
                    come = pool.compute_val(b * HALF_UNITS * 4 + 64 * (u // 2 + 1))
                    others, ones = pool.compute_val(b * UNITS + max(u - 1, 0)), pool.compute_val(b + 1)
                    read = pool.compute_val(b * SLOTS + CHUNKS * max(u - 1, 0))
                    settle(pool)
                    pool.wait_ge(x4_in[s], come)
                    pool.wait_ge(h1_mm, read)
                    pool.wait_ge(signed_ready, others)
                    pool.wait_ge(ones_col, ones)
                    pool.tensor_scalar(t0[HR:P, s, 0, :], x4[HR:P, s, :], 0.5, None, ALU.subtract)
                    pool.tensor_scalar(t0[HR:P, s, 1, :], x4[HR:P, s, :], 0.5, None, ALU.add).then_inc(x_side, 1)

                def tail(u):
                    s = u % 2
                    pool.wait_ge(lu_ready, b * UNITS + u + 1)
                    pool.wait_ge(sign_ready, b * UNITS + u)
                    pool.wait_ge(x_side, b * UNITS + min(u + 2, UNITS))
                    pool.tensor_tensor(lu_sum, lu[:, s, 0, :], lu[:, s, 1, :], ALU.add).then_inc(sum_ready, 1)
                    pool.wait_ge(sign_ready, b * UNITS + u + 1)
                    pool.wait_ge(sig_ready, b * UNITS + u)
                    pool.tensor_tensor(signed[:, 0, :], lu[:, s, 0, :], lu_sign, ALU.mult)
                    pool.tensor_tensor(signed[:, 1, :], lu[:, s, 1, :], lu_sign, ALU.mult).then_inc(signed_ready, 1)

                sides(0)
                sides(1)
                for u in range(UNITS):
                    if u >= 1 and u + 1 < UNITS:
                        sides(u + 1)
                    tail(u)

        @block.scalar
        def _(act):
            act.wait_ge(consts_in, CONST_DMAS * 16)
            act.activation(fth[:, :, :], fth[:, :, :], ACT.Tanh).then_inc(set_act, 1)
            act.wait_ge(set_step, 1)
            act.activation(sp_e[:, :, :], sp_abs[:, :, :], ACT.Exp, scale=-1.0).then_inc(set_act, 1)
            act.wait_ge(set_step, 2)
            act.activation(sp_l[:, :, :], sp_u[:, :, :], ACT.Ln).then_inc(set_act, 1)
            act.wait_ge(set_step, SETUP_STEPS)

            def deviation(b, k):
                act.wait_ge(stat_step, b * 2 * STAT_STEPS + k * STAT_STEPS + 6)
                act.activation(gstd[:, :], gvar[:, :], ACT.Sqrt).then_inc(stat_std, 1)

            with act.Fori(0, B) as b:
                deviation(b, 0)
                act.wait_ge(res_ready, b * UNITS)
                for s in range(2):
                    act.wait_ge(stored[s], b * HALF_UNITS)
                for n in range(4 * BLOCKS):
                    src = ps[:, n % 4, 0:N] if n < 2 * BLOCKS else ps[:, n % 4, 0:2 * C]
                    w = N if n < 2 * BLOCKS else 2 * C
                    col = (COL_BK if n < BLOCKS else COL_BQ)
                    act.wait_ge(proj_mm, b * 4 * BLOCKS + n + 1)
                    if n >= 2:
                        act.wait_ge(proj_val, b * 4 * BLOCKS + n - 1)
                    if n < 2 * BLOCKS:
                        act.activation(p_pos[:, n % 2, 0:w], src, ACT.Relu, bias=cols_sb[:, col:col + 1])
                        act.activation(p_neg[:, n % 2, 0:w], src, ACT.Relu, bias=ncols[:, col:col + 1],
                                       scale=-1.0).then_inc(proj_act, 1)
                    else:
                        act.activation(p_pos[:, n % 2, 0:w], src, ACT.Relu)
                        act.activation(p_neg[:, n % 2, 0:w], src, ACT.Relu, scale=-1.0).then_inc(proj_act, 1)

                def exps(pairs, q):
                    sc = ps[:, 2 * (q % 2):2 * (q % 2) + 2, :]
                    act.wait_ge(scored, pairs + q + 1)
                    if q >= 4:
                        act.wait_ge(summed, pairs + q - 3)
                    act.activation(e_hi[:, q % 4, :].rearrange("p (k n) -> p k n", k=2), sc, ACT.Exp)
                    if q >= 2:
                        act.wait_ge(lo_ready, pairs + q - 1)
                    act.activation(e_32[:, q % 2, :].rearrange("p (k n) -> p k n", k=2), sc,
                                   ACT.Exp).then_inc(full_ready, 1)

                def normalise(b, j, slot):
                    act.wait_ge(den_ready, b * BLOCKS + j + 1)
                    act.wait_ge(out_turn, b * 2 * BLOCKS + 2 * j)
                    for t in range(NT):
                        ins = act.activation(o_sb[:, slot, t, :],
                                             ps[:, own_banks(slot) + t // 2, (t % 2) * 256:(t % 2) * 256 + C],
                                             ACT.Copy, scale=rden[:, t:t + 1])
                    ins.then_inc(out_norm, 1)

                def body(before, parity, first, last):
                    pairs = act.compute_val(b * BLOCKS * PAIRS + before * PAIRS)
                    for p in range(PAIRS):
                        if p == 0 and not first:
                            normalise(b, before, 1 - parity)
                        if p + 2 < PAIRS or not last:
                            exps(pairs, (0 if first else PAIRS) + p + 2)

                pairs0 = act.compute_val(b * BLOCKS * PAIRS)
                exps(pairs0, 0)
                exps(pairs0, 1)
                body(0, 0, True, False)
                with act.Fori(0, (BLOCKS - 2) // 2) as jj:
                    body(act.compute_val(jj * 2), 1, False, False)
                    body(act.compute_val(jj * 2 + 1), 0, False, False)
                body(BLOCKS - 2, 1, False, True)
                normalise(b, BLOCKS - 1, 1)
                deviation(b, 1)

                def first_tanh(c):
                    u, k = c // CHUNKS, c % CHUNKS
                    s, g = u % 2, u // 2
                    if k == 0:
                        act.wait_ge(x4_in[s], b * HALF_UNITS * 4 + 64 * (u // 2 + 1))
                        act.wait_ge(h1_mm, b * SLOTS + CHUNKS * max(u - 1, 0))
                    for d, col in ((0, SC_BL), (1, SC_BU)):
                        ins = act.activation(t0[0:HR, s, d, k * N:(k + 1) * N], x4[0:HR, s, k * N:(k + 1) * N],
                                             ACT.Tanh, bias=w_all[0:HR, g, col:col + 1],
                                             scale=w_all[0:HR, g, SC_SP0:SC_SP0 + 1])
                    ins.then_inc(t0_ready, 1)

                def tanh(c, dst, bank, col, before, after):
                    g = c // CHUNKS // 2
                    act.wait_ge(before, b * SLOTS + c + 1)
                    act.activation(dst[0:HR, c % 2, :, :], ps[0:HR, bank:bank + 2, :], ACT.Tanh,
                                   bias=w_all[0:HR, g, col:col + 1]).then_inc(after, 1)

                def logits(u):
                    act.wait_ge(h3_mm, b * SLOTS + CHUNKS * (u + 1))
                    act.wait_ge(signed_ready, b * UNITS + max(u - 1, 0))
                    act.activation(lu[:, u % 2, :, :], ps[:, 6:8, :], ACT.Identity,
                                   bias=w_all[:, u // 2, SC_C3:SC_C3 + 1]).then_inc(lu_ready, 1)

                def sign(u):
                    act.wait_ge(sum_ready, b * UNITS + u + 1)
                    act.wait_ge(signed_ready, b * UNITS + u)
                    act.activation(lu_sign, lu_sum, ACT.Sign).then_inc(sign_ready, 1)

                def sigmoid(u):
                    act.wait_ge(signed_ready, b * UNITS + u + 1)
                    act.wait_ge(dif_ready, b * UNITS + u)
                    act.activation(sig[:, :, :], signed[:, :, :], ACT.Sigmoid, scale=-1.0).then_inc(sig_ready, 1)

                first_tanh(0)
                first_tanh(1)
                for s in range(SLOTS + 6):
                    if s < SLOTS:
                        tanh(s, t1, 2 * (s % 2), SC_C1, h1_mm, t1_ready)
                    if 1 <= s <= SLOTS:
                        tanh(s - 1, t2, 4, SC_C2, h2_mm, t2_ready)
                    if s + 2 < SLOTS:
                        first_tanh(s + 2)
                    u = (s - 5) // CHUNKS
                    if s >= 5 and u < UNITS:
                        if (s - 5) % CHUNKS == 0:
                            logits(u)
                        if (s - 5) % CHUNKS == 1:
                            sign(u)
                        if (s - 5) % CHUNKS == 2:
                            sigmoid(u)

        @block.vector
        def _(dve):
            steps = [0]

            def setup(ins):
                steps[0] += 1
                ins.then_inc(set_step, 1)
                dve.wait_ge(set_step, steps[0])

            def mul_add(acc, start, factors):
                for n, (a, c) in enumerate(factors):
                    setup(dve.tensor_tensor(prod[:, :], a, c, ALU.mult))
                    setup(dve.tensor_tensor(acc, start if n == 0 else acc, prod[:, :], ALU.add))

            dve.wait_ge(consts_in, CONST_DMAS * 16)
            setup(dve.scalar_tensor_tensor(sp_abs[:, :, :], msp[:, :, :], -1.0, msp[:, :, :], ALU.mult, ALU.max))
            dve.wait_ge(set_act, 2)
            setup(dve.tensor_scalar(sp_u[:, :, :], sp_e[:, :, :], 1.0, None, ALU.add))
            dve.wait_ge(set_act, 3)
            setup(dve.tensor_scalar(sp_abs[:, :, :], sp_u[:, :, :], 1.0, 1e-30, ALU.subtract, ALU.max))
            setup(dve.reciprocal(sp_abs[:, :, :], sp_abs[:, :, :]))
            setup(dve.tensor_tensor(sp_abs[:, :, :], sp_abs[:, :, :], sp_e[:, :, :], ALU.mult))
            setup(dve.tensor_tensor(sp_l[:, :, :], sp_l[:, :, :], sp_abs[:, :, :], ALU.mult))
            setup(dve.scalar_tensor_tensor(sp_u[:, :, :], sp_u[:, :, :], 1.0, sp_e[:, :, :], ALU.is_equal, ALU.mult))
            setup(dve.tensor_tensor(sp_l[:, :, :], sp_l[:, :, :], sp_u[:, :, :], ALU.add))
            setup(dve.scalar_tensor_tensor(msp[:, :, :], msp[:, :, :], 0.0, sp_l[:, :, :], ALU.max, ALU.add))
            for i in range(HID):
                setup(dve.tensor_tensor(coef[0:HR, :, i], msp[0:HR, :, M1C + i], fth[0:HR, :, F0O], ALU.mult))
                setup(dve.tensor_tensor(coef[HR:P, :, i], msp[HR:P, :, M1 + HID * i], msp[HR:P, :, M0], ALU.mult))
                for j in range(1, HID):
                    setup(dve.tensor_tensor(prod[HR:P, :], msp[HR:P, :, M1 + HID * i + j], msp[HR:P, :, M0 + j],
                                            ALU.mult))
                    setup(dve.tensor_tensor(coef[HR:P, :, i], coef[HR:P, :, i], prod[HR:P, :], ALU.add))
            for i in range(HID):
                mul_add(c1_all[:, :, i], bra[:, :, B1 + i],
                        [(msp[:, :, M1 + HID * i + j], bra[:, :, B0 + j]) for j in range(HID)])
            for i in range(HID):
                mul_add(c2_all[:, :, i], bra[:, :, B2 + i],
                        [(msp[:, :, M2 + HID * i + j], c1_all[:, :, j]) for j in range(HID)])
            mul_add(w_all[:, :, SC_C1], bra[:, :, B1O], [(msp[:, :, M1R + j], bra[:, :, B0 + j]) for j in range(HID)])
            mul_add(w_all[:, :, SC_C2], bra[:, :, B2O], [(msp[:, :, M2R + j], c1_all[:, :, j]) for j in range(HID)])
            mul_add(w_all[:, :, SC_C3], bra[:, :, B3], [(msp[:, :, M3 + j], c2_all[:, :, j]) for j in range(HID)])
            setup(dve.tensor_copy(w_all[:, :, SC_SP0], msp[:, :, M0R]))
            setup(dve.scalar_tensor_tensor(w_all[:, :, SC_BL], msp[:, :, M0R], -0.5, bra[:, :, B0O], ALU.mult, ALU.add))
            setup(dve.scalar_tensor_tensor(w_all[:, :, SC_BU], msp[:, :, M0R], 0.5, bra[:, :, B0O], ALU.mult, ALU.add))
            setup(dve.tensor_copy(w_all[:, :, SC_T1], fth[:, :, F1O]))
            setup(dve.tensor_copy(w_all[:, :, SC_T2], fth[:, :, F2O]))
            setup(dve.tensor_scalar(ncols[:, :], cols_sb[:, :], -1.0, None, ALU.mult))
            setup(dve.tensor_copy(eye16[:, :], eye_sb[:, :]))
            assert steps[0] == SETUP_STEPS, steps[0]

            with dve.Fori(0, B) as b:
                def groupnorm(k):
                    base = dve.compute_val(b * 2 * STAT_STEPS + k * STAT_STEPS)
                    n = [0]

                    def step(ins):
                        n[0] += 1
                        ins.then_inc(stat_step, 1)
                        dve.wait_ge(stat_step, base + n[0])

                    dve.bn_aggr(mv[:, 0, :], stats[:, 0, :, :])
                    step(dve.bn_aggr(mv[:, 1, :], stats[:, 1, :, :]))
                    dve.wait_ge(stat_mm, b * 4 + 2 * k + 1)
                    step(dve.tensor_copy(gmean[:, :], ps[0:HALF, 0, 0:2]))
                    step(dve.tensor_tensor(tmp_a[:, :], mv[:, :, 0], gmean[:, :], ALU.subtract))
                    step(dve.tensor_tensor(tmp_b[:, :], tmp_a[:, :], tmp_a[:, :], ALU.mult))
                    step(dve.tensor_tensor(tmp_a[:, :], tmp_b[:, :], mv[:, :, 1], ALU.add))
                    dve.wait_ge(stat_mm, b * 4 + 2 * k + 2)
                    step(dve.tensor_scalar(gvar[:, :], ps[0:HALF, 1, 0:2], EPS, None, ALU.add))
                    dve.wait_ge(stat_std, b * 2 + k + 1)
                    step(dve.reciprocal(rstd[:, :], gstd[:, :]))
                    step(dve.tensor_tensor(tmp_a[:, :], rstd[:, :], rstd[:, :], ALU.mult))
                    step(dve.tensor_tensor(tmp_b[:, :], tmp_a[:, :], gvar[:, :], ALU.mult))
                    step(dve.tensor_scalar(tmp_a[:, :], tmp_b[:, :], -0.5, 1.5, ALU.mult, ALU.add))
                    step(dve.tensor_tensor(rstd[:, :], rstd[:, :], tmp_a[:, :], ALU.mult))
                    assert n[0] == STAT_STEPS
                    for h in range(2):
                        dve.tensor_scalar(xn[0:HALF, h, :], x_sb[:, h, :], gmean[:, h:h + 1], rstd[:, h:h + 1],
                                          ALU.subtract, ALU.mult).then_inc(xn_ready, 1)

                dve.wait_ge(x_in, b * 32 + 32)
                for h in range(2):
                    for j in range(BLOCKS):
                        ins = dve.bn_stats(stats[:, h, j, :], x_sb[:, h, j * N:(j + 1) * N])
                ins.then_inc(x_stat, 1)
                stat_now, norm_stored = dve.compute_val(b + 1), dve.compute_val(b * 16)
                settle(dve)
                dve.wait_ge(x_stat, stat_now)
                for h in range(2):
                    dve.wait_ge(xn_out[h], norm_stored)
                groupnorm(0)

                def reduce(base, m):
                    dve.wait_ge(max_mm, base + m + 1)
                    dve.tensor_reduce(mxp[:, m // BLOCKS, m % BLOCKS:m % BLOCKS + 1], ps[:, 4 + bank_of[0] + m % 2, :],
                                      AX_X, ALU.max).then_inc(max_red, 1)

                bank_of = [0]

                def split_max(g, base):
                    st = dve.compute_val(g * MAX_STEPS)
                    n = [0]

                    def step(ins):
                        n[0] += 1
                        ins.then_inc(max_step, 1)
                        dve.wait_ge(max_step, st + n[0])

                    dve.wait_ge(max_red, base + MAXES)
                    step(dve.tensor_reduce(mx[:, :], mxp[:, :, :], AX_X, ALU.max))
                    step(dve.tensor_scalar(negm[:, :], mx[:, :], -1.0, ESHIFT, ALU.mult, ALU.add))
                    step(dve.tensor_scalar(mparts[:, 0, :], negm[:, :], 1.0 / BIG, None, ALU.mult))
                    step(dve.scalar_tensor_tensor(rest[:, :], mparts[:, 0, :], -BIG, negm[:, :], ALU.mult, ALU.add))
                    step(dve.tensor_copy(mparts[:, 1, :], rest[:, :]))
                    step(dve.tensor_tensor(mparts[:, 2, :], rest[:, :], mparts[:, 1, :], ALU.subtract))
                    assert n[0] == MAX_STEPS

                def rows_out(g, bank):
                    dve.wait_ge(max_turn, g + 1)
                    dve.wait_ge(max_in, g * 16)
                    dve.tensor_copy(mrows[:, :], ps[0:3 * NT, bank, 0:P // 2].bitcast(F16)).then_inc(max_rows, 1)

                blocks0 = dve.compute_val(b * BLOCKS)
                maxes0 = dve.compute_val(b * BLOCKS * MAXES)
                for n in range(4 * BLOCKS):
                    w = N if n < 2 * BLOCKS else 2 * C
                    col = COL_A2 if n < BLOCKS else COL_A1 if n < 2 * BLOCKS else COL_AA
                    s = n % 2
                    dve.wait_ge(proj_act, b * 4 * BLOCKS + n + 1)
                    dve.scalar_tensor_tensor(p_val[:, s, 0:w], p_neg[:, s, 0:w], ncols[:, col:col + 1],
                                             p_pos[:, s, 0:w], ALU.mult, ALU.add).then_inc(proj_val, 1)
                    dve.wait_ge(proj_val, b * 4 * BLOCKS + n + 1)
                    if n < 2 * BLOCKS:
                        st = (kst if n < BLOCKS else qst)[:, (n % BLOCKS) * N:(n % BLOCKS + 1) * N]
                        mask = COL_MK if n < BLOCKS else COL_MQ
                        dve.tensor_copy(p_hi[:, s, :], p_val[:, s, :]).then_inc(proj_hi, 1)
                        dve.wait_ge(proj_hi, b * 4 * BLOCKS + n + 1)
                        dve.scalar_tensor_tensor(st, p_hi[:, s, :], cols_sb[:, mask:mask + 1], p_val[:, s, :],
                                                 ALU.mult, ALU.add).then_inc(proj_done, 1)
                    else:
                        m = 2 * (n - 2 * BLOCKS)
                        val = p_val[:, s, 0:w].rearrange("p (k n) -> p k n", k=2)
                        dve.tensor_copy(v_sb[:, m:m + 2, 0:C], val).then_inc(proj_hi, 1)
                        dve.wait_ge(proj_hi, b * 4 * BLOCKS + n + 1)
                        dve.tensor_tensor(v_sb[:, m:m + 2, VW:VW + C], val, v_sb[:, m:m + 2, 0:C],
                                          ALU.subtract).then_inc(proj_done, 1)
                        reduce(maxes0, m)
                        reduce(maxes0, m + 1)
                split_max(blocks0, maxes0)
                rows_out(blocks0, own_banks(0))

                def low(pairs, q):
                    dve.wait_ge(full_ready, pairs + q + 1)
                    dve.tensor_tensor(e_lo[:, q % 4, :], e_32[:, q % 2, :], e_hi[:, q % 4, :],
                                      ALU.subtract).then_inc(lo_ready, 1)

                def denominators(j, bank):
                    dve.wait_ge(summed, b * BLOCKS * PAIRS + j * PAIRS + PAIRS)
                    dve.wait_ge(out_norm, b * BLOCKS + j)
                    sums = ps[:, bank:bank + 2, :].rearrange("p k (t n) -> p k t n", t=2)
                    dve.reciprocal(rden[:, :].rearrange("p (k t) -> p k t", k=2), sums[:, :, :, C]
                                   ).then_inc(den_ready, 1)

                def add_half(j, col, h, bank):
                    dve.wait_ge(out_turn, b * 2 * BLOCKS + 2 * j + h + 1)
                    xs = x_sb[:, h, bass.ds(col, N)]
                    dve.tensor_tensor(xs, ps[0:HALF, bank, :], xs, ALU.add).then_inc(x2_ready, 1)
                    dve.wait_ge(x2_ready, b * 2 * BLOCKS + 2 * j + h + 1)
                    dve.bn_stats(stats[:, h, bass.ds(j, 1), :].rearrange("p a n -> p (a n)"), xs).then_inc(x2_stat, 1)

                def body(before, parity, first, last):
                    j = before + (0 if first else 1)
                    pairs = dve.compute_val(b * BLOCKS * PAIRS + j * PAIRS)
                    maxes = dve.compute_val(b * BLOCKS * MAXES + j * MAXES + MAXES)
                    nxt = dve.compute_val(b * BLOCKS + j + 1)
                    col = dve.compute_val(before * N)
                    free = own_banks(1 - parity)
                    bank_of[0] = free - 4
                    for p in range(PAIRS):
                        if p == 0 and not first:
                            denominators(before, free)
                        if p == 12 and not last:
                            rows_out(nxt, free)
                        if p + 1 < PAIRS or not last:
                            low(pairs, p + 1)
                        if not last:
                            for m in range(PER_STEP * p, min(PER_STEP * (p + 1), MAXES)):
                                reduce(maxes, m)
                            if p == 11:
                                split_max(nxt, maxes)
                        if not first and p in (13, 14):
                            add_half(before, col, p - 13, free + 1 - (p - 13))

                low(dve.compute_val(b * BLOCKS * PAIRS), 0)
                body(0, 0, True, False)
                with dve.Fori(0, (BLOCKS - 2) // 2) as jj:
                    body(dve.compute_val(jj * 2), 1, False, False)
                    body(dve.compute_val(jj * 2 + 1), 0, False, False)
                body(BLOCKS - 2, 1, False, True)
                denominators(BLOCKS - 1, own_banks(1))
                for h in range(2):
                    add_half(BLOCKS - 1, (BLOCKS - 1) * N, h, own_banks(0) + 1 - h)
                settle(dve)
                dve.wait_ge(x2_stat, b * 2 * BLOCKS + 2 * BLOCKS)
                groupnorm(1)

                def gate(c, t, bank, dst, slots, col, before, read, reads, after):
                    dve.wait_ge(before, b * SLOTS + c + 1)
                    dve.wait_ge(read, b * SLOTS + reads)
                    dve.scalar_tensor_tensor(dst[0:HR, c % slots, :, :], t[0:HR, c % 2, :, :],
                                             w_all[0:HR, c // CHUNKS // 2, col:col + 1], ps[0:HR, bank:bank + 2, :],
                                             ALU.mult, ALU.add).then_inc(after, 1)

                def result(u):
                    s = u % 2
                    dve.wait_ge(sig_ready, b * UNITS + u + 1)
                    dve.tensor_tensor(dif, sig[:, 1, :], sig[:, 0, :], ALU.subtract).then_inc(dif_ready, 1)
                    dve.wait_ge(dif_ready, b * UNITS + u + 1)
                    dve.scalar_tensor_tensor(size, dif, -1.0, dif, ALU.mult, ALU.max).then_inc(size_ready, 1)
                    dve.wait_ge(size_ready, b * UNITS + u + 1)
                    dve.wait_ge(x2t_in[s], b * HALF_UNITS + 16 * (u // 2 + 1))
                    dve.wait_ge(stored[s], b * HALF_UNITS + 16 * (u // 2))
                    dve.scalar_tensor_tensor(res[:, s, :], size, 1e-6, x2t[:, s, :], ALU.max,
                                             ALU.add).then_inc(res_ready, 1)

                for s in range(SLOTS + 8):
                    if s < SLOTS:
                        gate(s, t1, 2 * (s % 2), h1, 2, SC_T1, t1_ready, h2_mm, max(s - 1, 0), h1_ready)
                    if 1 <= s <= SLOTS:
                        gate(s - 1, t2, 4, h2, 4, SC_T2, t2_ready, h3_mm, max(s - 4, 0), h2_ready)
                    if s >= 8 and (s - 8) % CHUNKS == 0 and (s - 8) // CHUNKS < UNITS:
                        result((s - 8) // CHUNKS)

        @block.tensor
        def _(pe):
            pe.wait_ge(consts_in, CONST_DMAS * 16)
            pe.wait_ge(set_gp, 2)
            with pe.Fori(0, B) as b:
                def averages(k):
                    pe.wait_ge(stat_step, b * 2 * STAT_STEPS + k * STAT_STEPS + 1)
                    pe.matmul(ps[0:HALF, 0, 0:2], g6_sb[:, :], mv[:, :, 0], start=True, stop=True
                              ).then_inc(stat_mm, 1)
                    pe.wait_ge(stat_step, b * 2 * STAT_STEPS + k * STAT_STEPS + 5)
                    pe.matmul(ps[0:HALF, 1, 0:2], g6_sb[:, :], tmp_a[:, :], start=True, stop=True
                              ).then_inc(stat_mm, 1)

                pe.wait_ge(lu_ready, b * UNITS)
                averages(0)
                pe.wait_ge(xn_ready, b * 4 + 2)

                def bank_free(n):
                    if n >= 4:
                        pe.wait_ge(proj_act, b * 4 * BLOCKS + n - 3)

                for n in range(2 * BLOCKS):
                    bank_free(n)
                    which = 1 if n < BLOCKS else 0
                    c0 = (n % BLOCKS) * N
                    for h in range(2):
                        ins = pe.matmul(ps[:, n % 4, :], wqk_sb[:, h, which, :], xn[0:HALF, h, c0:c0 + N],
                                        start=(h == 0), stop=(h == 1))
                    ins.then_inc(proj_mm, 1)

                def max_tile(base, q_col, m, bank, evacuated):
                    if m >= 2:
                        pe.wait_ge(max_red, base + m - 1)
                    elif evacuated is not None:
                        pe.wait_ge(out_norm, evacuated)
                    pe.matmul(ps[:, bank + m % 2, :], qst[:, bass.ds(q_col + (m // BLOCKS) * P, P)],
                              kst[:, (m % BLOCKS) * N:(m % BLOCKS + 1) * N], start=True, stop=True
                              ).then_inc(max_mm, 1)

                maxes0 = pe.compute_val(b * BLOCKS * MAXES)
                for v in range(2 * BLOCKS):
                    n = 2 * BLOCKS + v
                    bank_free(n)
                    for k in range(2):
                        m = 2 * v + k
                        pe.matmul(ps[:, n % 4, k * C:(k + 1) * C], xn[0:HALF, 0, m * P:(m + 1) * P],
                                  wv_sb[0:HALF, 0, :], start=True, stop=False)
                        ins = pe.matmul(ps[:, n % 4, k * C:(k + 1) * C], xn[:, 1, m * P:(m + 1) * P],
                                        wv_sb[:, 1, :], start=False, stop=True)
                    ins.then_inc(proj_mm, 1)
                    if v == 0:
                        pe.wait_ge(proj_done, b * 4 * BLOCKS + 2 * BLOCKS)
                    for m in (2 * v, 2 * v + 1):
                        max_tile(maxes0, 0, m, own_banks(0), None)

                def turn_max(g, bank):
                    pe.wait_ge(max_step, g * MAX_STEPS + MAX_STEPS)
                    pe.transpose(ps[0:3 * NT, bank, 0:P // 2].bitcast(F16), mparts[:, :, :]
                                 .rearrange("p r t -> p (r t)"), eye16[:, :]).then_inc(max_turn, 1)

                def turn_out(slot, h, bank):
                    for t in range(NT):
                        ins = pe.transpose(ps[0:HALF, bank, t * P:(t + 1) * P],
                                           o_sb[:, slot, t, h * HALF:(h + 1) * HALF], eye_sb[:, :])
                    ins.then_inc(out_turn, 1)

                def scores(pairs, q_col, q):
                    for i in range(2):
                        m = (2 * q + i) % MT
                        ins = pe.matmul(ps[:, 2 * (q % 2) + i, :], kst[:, m * P:(m + 1) * P],
                                        qst[:, bass.ds(q_col, N)], start=True, stop=True)
                    ins.then_inc(scored, 1)

                def body(before, parity, first, last):
                    j = before + (0 if first else 1)
                    pairs = pe.compute_val(b * BLOCKS * PAIRS + j * PAIRS)
                    maxes = pe.compute_val(b * BLOCKS * MAXES + j * MAXES + MAXES)
                    blocks = pe.compute_val(b * BLOCKS + j)
                    q_col = pe.compute_val(j * N)
                    q_next = pe.compute_val(j * N + N)
                    mine, free = own_banks(parity), own_banks(1 - parity)
                    for p in range(PAIRS):
                        if p == 12 and not last:
                            turn_max(blocks + 1, free)
                        if p + 2 < PAIRS or not last:
                            pe.wait_ge(full_ready, pairs + p + 1)
                            if p + 2 == PAIRS:
                                pe.wait_ge(max_in, blocks * 16 + 32)
                            scores(pairs, q_col if p + 2 < PAIRS else q_next, p + 2)
                        pe.wait_ge(lo_ready, pairs + p + 1)
                        if p == 0 and first:
                            pe.wait_ge(proj_done, b * 4 * BLOCKS + 4 * BLOCKS)
                            pe.wait_ge(ones_col, b + 1)
                        if p == 0 and not first:
                            pe.wait_ge(x2_ready, b * 2 * BLOCKS + 2 * before)
                        todo = list(range(PER_STEP * p, min(PER_STEP * (p + 1), MAXES))) if not last else []
                        spots = (5, 6, 7) if p == 0 else (2, 5, 7)
                        for i in range(2):
                            m = 2 * p + i
                            for t in range(NT):
                                eh = e_hi[:, p % 4, i * N + t * P:i * N + (t + 1) * P]
                                el = e_lo[:, p % 4, i * N + t * P:i * N + (t + 1) * P]
                                acc = ps[:, mine + t // 2, (t % 2) * 256:(t % 2) * 256 + C + 1]
                                pe.matmul(acc, eh, v_sb[:, m, 0:C + 1], start=(m == 0 and t % 2 == 0), stop=False,
                                          skip_group_check=True)
                                pe.matmul(acc[:, 0:C], eh, v_sb[:, m, VW:VW + C], start=False, stop=False,
                                          skip_group_check=True)
                                ins = pe.matmul(acc, el, v_sb[:, m, 0:C + 1], start=False, stop=(m == MT - 1),
                                                skip_group_check=True)
                                if i == 1 and t == NT - 1:
                                    ins.then_inc(summed, 1)
                                if i * NT + t in spots and todo:
                                    max_tile(maxes, q_next, todo.pop(0), free, blocks)
                        if not first and p in (12, 13):
                            if p == 12:
                                pe.wait_ge(out_norm, blocks)
                            elif not last:
                                pe.wait_ge(max_rows, blocks + 2)
                            turn_out(1 - parity, p - 12, free + 1 - (p - 12))

                turn_max(pe.compute_val(b * BLOCKS), own_banks(0))
                pe.wait_ge(max_in, b * BLOCKS * 16 + 16)
                pe.wait_ge(proj_act, b * 4 * BLOCKS + 4 * BLOCKS)
                pairs0 = pe.compute_val(b * BLOCKS * PAIRS)
                scores(pairs0, 0, 0)
                scores(pairs0, 0, 1)
                body(0, 0, True, False)
                with pe.Fori(0, (BLOCKS - 2) // 2) as jj:
                    body(pe.compute_val(jj * 2), 1, False, False)
                    body(pe.compute_val(jj * 2 + 1), 0, False, False)
                body(BLOCKS - 2, 1, False, True)
                pe.wait_ge(out_norm, b * BLOCKS + BLOCKS)
                pe.wait_ge(x2_ready, b * 2 * BLOCKS + 2 * BLOCKS - 2)
                for h in range(2):
                    turn_out(1, h, own_banks(0) + 1 - h)
                averages(1)

                def product(c, banks, w0, w1, k_rows, src, sems, after):
                    g = c // CHUNKS // 2
                    for d in range(2):
                        ins = pe.matmul(ps[0:w1 - w0, banks + d, :], w_all[0:k_rows, g, w0:w1], src(d),
                                        start=True, stop=True)
                    ins.then_inc(after, 1)

                for s in range(SLOTS + 2):
                    if s < SLOTS:
                        u, k = s // CHUNKS, s % CHUNKS
                        pe.wait_ge(t0_ready, b * SLOTS + s + 1)
                        if k == 0:
                            pe.wait_ge(x_side, b * UNITS + u + 1)
                        pe.wait_ge(h1_ready, b * SLOTS + max(s - 1, 0))
                        for d in range(2):
                            ins = pe.matmul(ps[0:HR, 2 * (s % 2) + d, :], w_all[:, u // 2, 0:HR],
                                            t0[:, u % 2, d, k * N:(k + 1) * N], start=True, stop=True)
                        ins.then_inc(h1_mm, 1)
                    if 1 <= s <= SLOTS:
                        c = s - 1
                        pe.wait_ge(h1_ready, b * SLOTS + c + 1)
                        pe.wait_ge(h2_ready, b * SLOTS + c)
                        for d in range(2):
                            ins = pe.matmul(ps[0:HR, 4 + d, :], w_all[0:HR, c // CHUNKS // 2, HR:2 * HR],
                                            h1[0:HR, c % 2, d, :], start=True, stop=True)
                        ins.then_inc(h2_mm, 1)
                    if s >= 2:
                        c = s - 2
                        u, k = c // CHUNKS, c % CHUNKS
                        pe.wait_ge(h2_ready, b * SLOTS + c + 1)
                        if k == 0:
                            pe.wait_ge(lu_ready, b * UNITS + u)
                        for d in range(2):
                            ins = pe.matmul(ps[k * G:(k + 1) * G, 6 + d, :], w_all[0:HR, u // 2, 2 * HR:WCOLS],
                                            h2[0:HR, c % 4, d, :], start=True, stop=True)
                        ins.then_inc(h3_mm, 1)


def layout(inputs):
    import numpy as np
    a = {k: np.asarray(v) for k, v in inputs.items()}
    f = np.float32
    wqk = np.zeros((C, 2, P), f)
    cols = np.zeros((P, NCOLS), f)
    for k in range(P // SUB):
        wqk[:, 0, k * SUB:k * SUB + CR] = a["L0_conv_w1"].T
        wqk[:, 1, k * SUB:k * SUB + CR] = a["L0_conv_w2"].T
        cols[k * SUB:k * SUB + CR, COL_BQ] = a["L0_conv_b1"]
        cols[k * SUB:k * SUB + CR, COL_BK] = a["L0_conv_b2"]
    cols[CR:CR + 3, COL_BK] = (BIG, 1.0, 1.0)
    cols[:, COL_A1], cols[:, COL_A2], cols[:, COL_AA] = a["L0_conv_a1"], a["L0_conv_a2"], a["L0_conv_aa"]
    cols[2 * SUB:, COL_MQ] = -1.0
    cols[SUB:2 * SUB, COL_MK] = cols[3 * SUB:, COL_MK] = -1.0
    wv = np.concatenate([a["L0_conv_wa"].T, a["L0_conv_ba"][None, :]], 0)
    per = C // 32
    g6 = np.kron(np.eye(HALF // per, dtype=f), np.full((per, per), 1.0 / per, f))
    diag = np.tile(np.eye(G, dtype=f), (4, 1))

    def rows(of):
        parts = [of(min(j, HID - 1)).reshape(GROUPS, G, -1).transpose(1, 0, 2) for j in range(4)]
        return np.ascontiguousarray(np.concatenate(parts, 0))

    m0, m1, m2, m3 = (a[f"L1_conv_m{i}"] for i in range(4))
    b0, b1, b2, b3 = (a[f"L1_conv_b{i}"][:, :, 0] for i in range(4))
    f0, f1, f2 = (a[f"L1_conv_f{i}"][:, :, 0] for i in range(3))
    mraw = rows(lambda j: np.concatenate([
        m0[:, :, 0], m1.reshape(C, 9), m2.reshape(C, 9), m3[:, 0, :],
        m1[:, :, j], m2[:, :, j], m3[:, 0, j:j + 1], m0[:, j], m1[:, j, :], m2[:, j, :]], 1))
    fraw = rows(lambda j: np.stack([f0[:, j], f1[:, j], f2[:, j]], 1))
    braw = rows(lambda j: np.concatenate([b0, b1, b2, b3, b0[:, j:j + 1], b1[:, j:j + 1], b2[:, j:j + 1]], 1))
    return {"x": np.ascontiguousarray(a["x"]), "wqk": wqk, "wv": np.ascontiguousarray(wv), "cols": cols, "g6": g6,
            "eye": np.eye(P, dtype=f), "diag": diag, "mraw": mraw, "fraw": fraw, "braw": braw}


def kernel(**inputs):
    import concourse.bacc as bacc
    from concourse.bass_utils import run_bass_kernel_spmd

    nc = bacc.Bacc("TRN2", target_bir_lowering=False, num_devices=1)
    arrays = layout(inputs)
    args = [nc.dram_tensor(f"{name}_dram", a.shape, mybir.dt.from_np(a.dtype), kind="ExternalInput").ap()
            for name, a in arrays.items()]
    out = nc.dram_tensor("out_dram", arrays["x"].shape, F32, kind="ExternalOutput").ap()
    x2_dram = nc.dram_tensor("x2_dram", (B * C, HW), F32).ap()
    xn_dram = nc.dram_tensor("xn_dram", (B * C, HW), F32).ap()
    program(nc, *args, out, x2_dram, xn_dram)
    r = run_bass_kernel_spmd(nc, [{f"{name}_dram": a for name, a in arrays.items()}], core_ids=[0])
    return r.results[0]["out_dram"]
```

```python
from contextlib import ExitStack

import concourse.bass as bass
from concourse import mybir

ALU = mybir.AluOpType
ACT = mybir.ActivationFunctionType
F32 = mybir.dt.float32
F16 = mybir.dt.float16
AX_X = mybir.AxisListType.X

B, C, HW = 8, 192, 64 * 64
CR = C // 8
P = 128
HALF = C // 2
N = 512
BLOCKS = HW // N
NT = N // P
MT = HW // P
PAIRS = MT // 2
MAXES = NT * BLOCKS
SUB = 32
VW = C + 2
EPS = 1e-5
LN2 = 0.6931471805599453
ESHIFT = 14 * LN2
BIG = 4096.0
PER_STEP = 3

COL_BQ, COL_BK, COL_A1, COL_A2, COL_AA, COL_MQ, COL_MK = range(7)
NCOLS = 7
CONST_DMAS = 10

G = 32
GROUPS = C // G
HID = 3
HR = HID * G
CHUNKS = 4
UN = CHUNKS * N
WCOLS = HR + HR + G
SC_SP0, SC_BL, SC_BU, SC_C1, SC_C2, SC_T1, SC_T2, SC_C3 = range(WCOLS, WCOLS + 8)
WROW = WCOLS + 8
UNITS = 2 * GROUPS
SLOTS = UNITS * CHUNKS

M0, M1, M2, M3 = 0, 3, 12, 21
M1C, M2C, M3C = 24, 27, 30
M0R, M1R, M2R = 31, 32, 35
NM = 38
F0O, F1O, F2O = 0, 1, 2
NF = 3
B0, B1, B2, B3, B0O, B1O, B2O = 0, 3, 6, 9, 10, 11, 12
NB = 13

SETUP_STEPS = 9 + 3 * 6 + 9 * 6 + 7
STAT_STEPS = 11
H2_SLOTS = 4
START = 1
MAX_STEPS = 6
FIRST_MAX = 2
FIRST_SPLIT = FIRST_MAX + -(-MAXES // PER_STEP)


def first_maxes(v):
    start = PER_STEP * (v - FIRST_MAX)
    return range(max(start, 0), min(max(start + PER_STEP, 0), MAXES))


def program(nc, x, wqk, wv, cols, g6, eye, diag, mraw, fraw, braw, out):
    x_rows = x.rearrange("b c h w -> (b c) (h w)")
    out_rows = out.rearrange("b c h w -> (b c) (h w)")
    with ExitStack() as ctx:
        def sb(name, shape, dt=F32):
            return ctx.enter_context(nc.sbuf_tensor(name, shape, dt))

        def sem(name):
            return ctx.enter_context(nc.semaphore(name))

        x_sb = sb("x_sb", [HALF, 2, HW])
        xn = sb("xn", [HALF + 1, 2, HW])
        wqk_sb = sb("wqk_sb", [HALF, 2, 2, P])
        wv_sb = sb("wv_sb", [HALF + 1, 2, C])
        cols_sb = sb("cols_sb", [P, NCOLS])
        ncols = sb("ncols", [P, NCOLS])
        g6_sb = sb("g6_sb", [HALF, HALF])
        eye_sb = sb("eye_sb", [P, P])
        eye16 = sb("eye16", [P, P], F16)
        diag_sb = sb("diag_sb", [P, G])
        stats = sb("stats", [HALF, 2, BLOCKS, 6])
        mv = sb("mv", [HALF, 2, 2])
        gmean = sb("gmean", [HALF, 2])
        gvar = sb("gvar", [HALF, 2])
        gstd = sb("gstd", [HALF, 2])
        rstd = sb("rstd", [HALF, 2])
        tmp_a = sb("tmp_a", [HALF, 2])
        tmp_b = sb("tmp_b", [HALF, 2])
        mxp = sb("mxp", [P, NT, BLOCKS])
        mx = sb("mx", [P, NT])
        negm = sb("negm", [P, NT])
        rest = sb("rest", [P, NT])
        mparts = sb("mparts", [P, 3, NT], F16)
        mrows = sb("mrows", [3 * NT, P], F16)
        rden = sb("rden", [P, NT])
        w_all = sb("w_all", [P, GROUPS, WROW])
        msp = sb("msp", [P, GROUPS, NM])
        fth = sb("fth", [P, GROUPS, NF])
        bra = sb("bra", [P, GROUPS, NB])
        sp_abs = sb("sp_abs", [P, GROUPS, NM])
        sp_e = sb("sp_e", [P, GROUPS, NM])
        sp_u = sb("sp_u", [P, GROUPS, NM])
        sp_l = sb("sp_l", [P, GROUPS, NM])
        coef = sb("coef", [P, GROUPS, HID])
        c1_all = sb("c1_all", [P, GROUPS, HID])
        c2_all = sb("c2_all", [P, GROUPS, HID])
        prod = sb("prod", [P, GROUPS])

        arena = sb("arena", [P, 30720])
        place = [0]

        def take(words):
            place[0] += words
            return arena[:, place[0] - words:place[0]]

        kst = take(HW // 2).bitcast(F16)
        qst = take(HW // 2).bitcast(F16)
        v_sb = take(MT * (VW + C) // 2).bitcast(F16).rearrange("p (m n) -> p m n", m=MT)
        e_hi = take(4 * N).bitcast(F16).rearrange("p (s n) -> p s n", s=4)
        e_lo = take(4 * N).bitcast(F16).rearrange("p (s n) -> p s n", s=4)
        e_32 = take(2 * 2 * N).rearrange("p (s n) -> p s n", s=2)
        o_sb = take(2 * NT * C).rearrange("p (s t n) -> p s t n", s=2, t=NT)
        p_pos = take(2 * N).rearrange("p (s n) -> p s n", s=2)
        p_neg = take(2 * N).rearrange("p (s n) -> p s n", s=2)
        p_val = take(2 * N).rearrange("p (s n) -> p s n", s=2)
        p_hi = take(N).bitcast(F16).rearrange("p (s n) -> p s n", s=2)
        place[0] = 0
        x4 = take(2 * UN).rearrange("p (s n) -> p s n", s=2)
        t0 = take(2 * 2 * UN).rearrange("p (s d n) -> p s d n", s=2, d=2)
        t1 = take(2 * 2 * N).rearrange("p (s d n) -> p s d n", s=2, d=2)
        t2 = take(2 * 2 * N).rearrange("p (s d n) -> p s d n", s=2, d=2)
        h1 = take(2 * 2 * N).rearrange("p (s d n) -> p s d n", s=2, d=2)
        h2 = take(H2_SLOTS * 2 * N).rearrange("p (s d n) -> p s d n", s=H2_SLOTS, d=2)
        lu = take(2 * 2 * N).rearrange("p (s d n) -> p s d n", s=2, d=2)
        lu_sum = take(N)
        lu_sign = take(N)
        signed = take(2 * N).rearrange("p (d n) -> p d n", d=2)
        sig = take(2 * N).rearrange("p (d n) -> p d n", d=2)
        dif = take(N)
        size = take(N)
        res = take(2 * N).rearrange("p (s n) -> p s n", s=2)
        x2t = take(2 * N).rearrange("p (s n) -> p s n", s=2)

        ps = ctx.enter_context(nc.psum_tensor("ps", [P, 8, N], F32))

        def own_banks(g):
            return 4 + 2 * (g % 2)

        consts_in = sem("consts_in")
        set_step = sem("set_step")
        set_act = sem("set_act")
        set_gp = sem("set_gp")
        ones_col = sem("ones_col")
        x_in = [sem(f"x_in{h}") for h in range(2)]
        x_stat = sem("x_stat")
        stat_step = sem("stat_step")
        stat_mm = sem("stat_mm")
        stat_std = sem("stat_std")
        xn_ready = sem("xn_ready")
        proj_mm = sem("proj_mm")
        proj_act = sem("proj_act")
        proj_val = sem("proj_val")
        qk_hi = sem("qk_hi")
        qk_done = sem("qk_done")
        v_hi = sem("v_hi")
        v_done = sem("v_done")
        max_mm = sem("max_mm")
        max_red = sem("max_red")
        max_step = sem("max_step")
        max_turn = sem("max_turn")
        max_rows = sem("max_rows")
        max_in = sem("max_in")
        scored = sem("scored")
        full_ready = sem("full_ready")
        lo_ready = sem("lo_ready")
        summed = sem("summed")
        den_ready = sem("den_ready")
        out_norm = sem("out_norm")
        out_turn = sem("out_turn")
        x2_ready = sem("x2_ready")
        x2_stat = sem("x2_stat")
        x4_in = [sem(f"x4_in{s}") for s in range(2)]
        x2t_in = [sem(f"x2t_in{s}") for s in range(2)]
        x_side = sem("x_side")
        t0_ready = sem("t0_ready")
        h1_mm = sem("h1_mm")
        t1_ready = sem("t1_ready")
        h1_ready = sem("h1_ready")
        h2_mm = sem("h2_mm")
        t2_ready = sem("t2_ready")
        h2_ready = sem("h2_ready")
        h3_mm = sem("h3_mm")
        lu_ready = sem("lu_ready")
        sum_ready = sem("sum_ready")
        sign_ready = sem("sign_ready")
        signed_ready = sem("signed_ready")
        sig_ready = sem("sig_ready")
        dif_ready = sem("dif_ready")
        size_ready = sem("size_ready")
        res_ready = sem("res_ready")
        stored = [sem(f"stored{s}") for s in range(2)]

        HALF_UNITS = UNITS // 2 * 16

        def settle(eng):
            eng.wait_ge(consts_in, CONST_DMAS * 16)
        block = ctx.enter_context(nc.Block())

        @block.sync
        def _(sp):
            for h in range(2):
                sp.dma_start(x_sb[:, h, :], x_rows[h * HALF:(h + 1) * HALF, :]).then_inc(x_in[h], 16)
            for dst, src in ((cols_sb[:, :], cols), (g6_sb[:, :], g6),
                             (wqk_sb[:, :, :, :], wqk.rearrange("(h p) k n -> p h k n", h=2)),
                             (wv_sb[0:HALF, :, :], wv[0:C, :].rearrange("(h p) n -> p h n", h=2)),
                             (wv_sb[HALF:HALF + 1, 1, :], wv[C:C + 1, :]),
                             (eye_sb[:, :], eye), (diag_sb[:, :], diag), (msp[:, :, :], mraw),
                             (fth[:, :, :], fraw), (bra[:, :, :], braw)):
                sp.dma_start(dst, src).then_inc(consts_in, 16)

            def image(b, row, last):
                sp.wait_ge(max_rows, b * BLOCKS + 1)
                sp.dma_start(qst[CR:CR + 3, 0:N].rearrange("r (t n) -> r t n", t=NT),
                             mrows[:, :]).then_inc(max_in, 16)
                with sp.Fori(1, BLOCKS) as j:
                    col = sp.compute_val(j * N)
                    sp.wait_ge(max_rows, b * BLOCKS + j + 1)
                    sp.dma_start(qst[CR:CR + 3, bass.ds(col, N)].rearrange("r (t n) -> r t n", t=NT),
                                 mrows[:, :]).then_inc(max_in, 16)
                for u in range(UNITS):
                    s, half = u % 2, u // (UNITS // 2)
                    rows = slice((u // 2) * G - half * HALF, (u // 2) * G - half * HALF + G)
                    if u % (UNITS // 2) == 0:
                        sp.wait_ge(xn_ready, b * 4 + 3 + half)
                    if u >= 2:
                        tanh_read = sp.compute_val(b * (SLOTS // 2) + (u - 1) * CHUNKS // 2)
                        side_read = sp.compute_val(b * UNITS + u - 1)
                        settle(sp)
                        sp.wait_ge(t0_ready, tanh_read)
                        sp.wait_ge(x_side, side_read)
                    for k in range(4):
                        sp.dma_start(x4[k * G:(k + 1) * G, s, :], xn[rows, half, s * UN:(s + 1) * UN]
                                     ).then_inc(x4_in[s], 16)
                    if u >= 3:
                        store(b, row, u - 3)
                    if u >= 1:
                        load_x2(b, u - 1)
                    if u == UNITS // 2 + 1 and not last:
                        next_x(b, row, 0)
                store(b, row, UNITS - 3)
                load_x2(b, UNITS - 1)
                if not last:
                    next_x(b, row, 1)
                store(b, row, UNITS - 2)
                store(b, row, UNITS - 1)

            def load_x2(b, u):
                s, half = u % 2, u // (UNITS // 2)
                c0 = (u // 2) * G - half * HALF
                for k in range(CHUNKS):
                    sp.dma_start(x2t[k * G:(k + 1) * G, s, :],
                                 x_sb[c0:c0 + G, half, s * UN + k * N:s * UN + (k + 1) * N]).then_inc(x2t_in[s], 16)

            def next_x(b, row, h):
                come = sp.compute_val(b * HALF_UNITS * CHUNKS + (h + 1) * HALF_UNITS // 2 * CHUNKS)
                settle(sp)
                for s in range(2):
                    sp.wait_ge(x2t_in[s], come)
                sp.dma_start(x_sb[:, h, :], x_rows[bass.ds(row + (2 + h) * HALF, HALF), :]).then_inc(x_in[h], 16)

            def store(b, row, u):
                sp.wait_ge(res_ready, b * UNITS + u + 1)
                sp.dma_start(out_rows[bass.ds(row + (u // 2) * G, G), (u % 2) * UN:(u % 2 + 1) * UN]
                             .rearrange("c (k n) -> k c n", k=CHUNKS), res[:, u % 2, :]).then_inc(stored[u % 2], 16)

            with sp.Fori(0, B - 1) as b:
                image(b, sp.compute_val(b * C), False)
            image(B - 1, (B - 1) * C, True)
            for s in range(2):
                sp.wait_ge(stored[s], B * HALF_UNITS)

        @block.gpsimd
        def _(pool):
            for counted in (out_norm, out_turn, x2_ready):
                pool.sem_inc(counted, START)
            pool.memset(xn[HALF:HALF + 1, :, :], 1.0).then_inc(set_gp, 1)
            pool.wait_ge(set_gp, 1)
            pool.wait_ge(set_step, SETUP_STEPS)
            for g in range(GROUPS):
                for i in range(HID):
                    pool.tensor_scalar(w_all[:, g, i * G:(i + 1) * G], diag_sb[:, :], coef[:, g, i:i + 1], None,
                                       ALU.mult)
                    pool.tensor_scalar(w_all[0:HR, g, HR + i * G:HR + (i + 1) * G], diag_sb[0:HR, :],
                                       msp[0:HR, g, M2C + i:M2C + i + 1], None, ALU.mult)
                ins = pool.tensor_scalar(w_all[0:HR, g, 2 * HR:WCOLS], diag_sb[0:HR, :],
                                         msp[0:HR, g, M3C:M3C + 1], None, ALU.mult)
            ins.then_inc(set_gp, 1)
            with pool.Fori(0, B) as b:
                pool.memset(v_sb[:, :, C:VW], 1.0).then_inc(ones_col, 1)
                for n in range(2 * BLOCKS):
                    pool.wait_ge(v_hi, b * 2 * BLOCKS + n + 1)
                    pool.tensor_tensor(v_sb[:, 2 * n:2 * n + 2, VW:VW + C],
                                       p_val[:, n % 2, 0:2 * C].rearrange("p (k n) -> p k n", k=2),
                                       v_sb[:, 2 * n:2 * n + 2, 0:C], ALU.subtract).then_inc(v_done, 1)

                def tail(u):
                    s = u % 2
                    pool.wait_ge(lu_ready, b * UNITS + u + 1)
                    if u >= 1:
                        pool.wait_ge(sign_ready, b * UNITS + u)
                    pool.tensor_tensor(lu_sum, lu[:, s, 0, :], lu[:, s, 1, :], ALU.add).then_inc(sum_ready, 1)
                    pool.wait_ge(sign_ready, b * UNITS + u + 1)
                    if u >= 1:
                        pool.wait_ge(sig_ready, b * UNITS + u)
                    pool.tensor_tensor(signed[:, 0, :], lu[:, s, 0, :], lu_sign, ALU.mult)
                    pool.tensor_tensor(signed[:, 1, :], lu[:, s, 1, :], lu_sign, ALU.mult).then_inc(signed_ready, 1)

                for u in range(UNITS):
                    tail(u)

        @block.scalar
        def _(act):
            act.wait_ge(consts_in, CONST_DMAS * 16)
            act.activation(fth[:, :, :], fth[:, :, :], ACT.Tanh).then_inc(set_act, 1)
            act.wait_ge(set_step, 1)
            act.activation(sp_e[:, :, :], sp_abs[:, :, :], ACT.Exp, scale=-1.0).then_inc(set_act, 1)
            act.wait_ge(set_step, 2)
            act.activation(sp_l[:, :, :], sp_u[:, :, :], ACT.Ln).then_inc(set_act, 1)
            act.wait_ge(set_step, SETUP_STEPS)

            def deviation(b, k):
                act.wait_ge(stat_step, b * 2 * STAT_STEPS + k * STAT_STEPS + 6)
                act.activation(gstd[:, :], gvar[:, :], ACT.Sqrt).then_inc(stat_std, 1)

            def image(b, last):
                for n in range(2 * BLOCKS):
                    col = (COL_BK if n < BLOCKS else COL_BQ)
                    act.wait_ge(proj_mm, b * 4 * BLOCKS + n + 1)
                    if n >= 2:
                        act.wait_ge(proj_val, b * 4 * BLOCKS + n - 1)
                    act.activation(p_pos[:, n % 2, :], ps[:, n % 4, :], ACT.Relu, bias=cols_sb[:, col:col + 1])
                    act.activation(p_neg[:, n % 2, :], ps[:, n % 4, :], ACT.Relu, bias=ncols[:, col:col + 1],
                                   scale=-1.0).then_inc(proj_act, 1)
                for v in range(2 * BLOCKS + 1):
                    n = 2 * BLOCKS + v
                    if v < 2 * BLOCKS:
                        act.wait_ge(proj_mm, b * 4 * BLOCKS + n + 1)
                        act.wait_ge(proj_val, b * 4 * BLOCKS + n - 1)
                        act.activation(p_pos[:, n % 2, 0:2 * C], ps[:, n % 4, 0:2 * C], ACT.Relu)
                        act.activation(p_neg[:, n % 2, 0:2 * C], ps[:, n % 4, 0:2 * C], ACT.Relu,
                                       scale=-1.0).then_inc(proj_act, 1)
                    if v >= 1:
                        act.wait_ge(proj_val, b * 4 * BLOCKS + n)
                        act.activation(v_sb[:, 2 * v - 2:2 * v, 0:C],
                                       p_val[:, (n - 1) % 2, 0:2 * C].rearrange("p (k n) -> p k n", k=2),
                                       ACT.Copy).then_inc(v_hi, 1)

                def exps(pairs, q):
                    sc = ps[:, 2 * (q % 2):2 * (q % 2) + 2, :]
                    act.wait_ge(scored, pairs + q + 1)
                    if q >= 4:
                        act.wait_ge(summed, pairs + q - 3)
                    act.activation(e_hi[:, q % 4, :].rearrange("p (k n) -> p k n", k=2), sc, ACT.Exp)
                    if q >= 2:
                        act.wait_ge(lo_ready, pairs + q - 1)
                    act.activation(e_32[:, q % 2, :].rearrange("p (k n) -> p k n", k=2), sc,
                                   ACT.Exp).then_inc(full_ready, 1)

                def normalise(b, j, slot):
                    act.wait_ge(den_ready, b * BLOCKS + j + 1)
                    act.wait_ge(out_turn, b * 2 * BLOCKS + 2 * j + START)
                    for t in range(NT):
                        ins = act.activation(o_sb[:, slot, t, :],
                                             ps[:, own_banks(slot) + t // 2, (t % 2) * 256:(t % 2) * 256 + C],
                                             ACT.Copy, scale=rden[:, t:t + 1])
                    ins.then_inc(out_norm, 1)

                def body(before, parity, first, last):
                    pairs = act.compute_val(b * BLOCKS * PAIRS + before * PAIRS)
                    for p in range(PAIRS):
                        if p == 0 and not first:
                            normalise(b, before, 1 - parity)
                        if p + 2 < PAIRS or not last:
                            exps(pairs, (0 if first else PAIRS) + p + 2)

                pairs0 = act.compute_val(b * BLOCKS * PAIRS)
                exps(pairs0, 0)
                exps(pairs0, 1)
                body(0, 0, True, False)
                with act.Fori(0, (BLOCKS - 2) // 2) as jj:
                    body(act.compute_val(jj * 2), 1, False, False)
                    body(act.compute_val(jj * 2 + 1), 0, False, False)
                body(BLOCKS - 2, 1, False, True)
                normalise(b, BLOCKS - 1, 1)
                deviation(b, 1)

                def first_tanh(c):
                    u, k = c // CHUNKS, c % CHUNKS
                    s, g = u % 2, u // 2
                    if k == 0:
                        act.wait_ge(x4_in[s], b * HALF_UNITS * 4 + 64 * (u // 2 + 1))
                        if u >= 2:
                            act.wait_ge(h1_mm, b * SLOTS + CHUNKS * (u - 1))
                    for d, col in ((0, SC_BL), (1, SC_BU)):
                        ins = act.activation(t0[0:HR, s, d, k * N:(k + 2) * N], x4[0:HR, s, k * N:(k + 2) * N],
                                             ACT.Tanh, bias=w_all[0:HR, g, col:col + 1],
                                             scale=w_all[0:HR, g, SC_SP0:SC_SP0 + 1])
                    ins.then_inc(t0_ready, 1)

                def tanh(c, dst, bank, col, before, after):
                    g = c // CHUNKS // 2
                    act.wait_ge(before, b * SLOTS + c + 1)
                    act.activation(dst[0:HR, c % 2, :, :], ps[0:HR, bank:bank + 2, :], ACT.Tanh,
                                   bias=w_all[0:HR, g, col:col + 1]).then_inc(after, 1)

                def logits(u):
                    act.wait_ge(h3_mm, b * UNITS + u + 1)
                    if u >= 2:
                        act.wait_ge(signed_ready, b * UNITS + u - 1)
                    act.activation(lu[:, u % 2, :, :], ps[:, 6:8, :], ACT.Identity,
                                   bias=w_all[:, u // 2, SC_C3:SC_C3 + 1]).then_inc(lu_ready, 1)

                def sign(u):
                    act.wait_ge(sum_ready, b * UNITS + u + 1)
                    if u >= 1:
                        act.wait_ge(signed_ready, b * UNITS + u)
                    act.activation(lu_sign, lu_sum, ACT.Sign).then_inc(sign_ready, 1)

                def sigmoid(u):
                    act.wait_ge(signed_ready, b * UNITS + u + 1)
                    if u >= 1:
                        act.wait_ge(dif_ready, b * UNITS + u)
                    act.activation(sig[:, :, :], signed[:, :, :], ACT.Sigmoid, scale=-1.0).then_inc(sig_ready, 1)

                first_tanh(0)
                for s in range(SLOTS + 6):
                    if s < SLOTS:
                        tanh(s, t1, 2 * (s % 3), SC_C1, h1_mm, t1_ready)
                    if 1 <= s <= SLOTS:
                        tanh(s - 1, t2, 2 * ((s - 1) % 3), SC_C2, h2_mm, t2_ready)
                    if s % 2 == 0 and s + 2 < SLOTS:
                        first_tanh(s + 2)
                    u = (s - 5) // CHUNKS
                    if s >= 5 and u < UNITS:
                        if (s - 5) % CHUNKS == 0:
                            logits(u)
                        if (s - 5) % CHUNKS == 1:
                            sign(u)
                        if (s - 5) % CHUNKS == 2:
                            sigmoid(u)
                if not last:
                    deviation(act.compute_val(b + 1), 0)

            deviation(0, 0)
            with act.Fori(0, B - 1) as b:
                image(b, False)
            image(B - 1, True)

        @block.vector
        def _(dve):
            steps = [0]

            def setup(ins):
                steps[0] += 1
                ins.then_inc(set_step, 1)
                dve.wait_ge(set_step, steps[0])

            def mul_add(acc, start, factors):
                for n, (a, c) in enumerate(factors):
                    setup(dve.tensor_tensor(prod[:, :], a, c, ALU.mult))
                    setup(dve.tensor_tensor(acc, start if n == 0 else acc, prod[:, :], ALU.add))

            dve.wait_ge(consts_in, CONST_DMAS * 16)
            setup(dve.scalar_tensor_tensor(sp_abs[:, :, :], msp[:, :, :], -1.0, msp[:, :, :], ALU.mult, ALU.max))
            dve.wait_ge(set_act, 2)
            setup(dve.tensor_scalar(sp_u[:, :, :], sp_e[:, :, :], 1.0, None, ALU.add))
            dve.wait_ge(set_act, 3)
            setup(dve.tensor_scalar(sp_abs[:, :, :], sp_u[:, :, :], 1.0, 1e-30, ALU.subtract, ALU.max))
            setup(dve.reciprocal(sp_abs[:, :, :], sp_abs[:, :, :]))
            setup(dve.tensor_tensor(sp_abs[:, :, :], sp_abs[:, :, :], sp_e[:, :, :], ALU.mult))
            setup(dve.tensor_tensor(sp_l[:, :, :], sp_l[:, :, :], sp_abs[:, :, :], ALU.mult))
            setup(dve.scalar_tensor_tensor(sp_u[:, :, :], sp_u[:, :, :], 1.0, sp_e[:, :, :], ALU.is_equal, ALU.mult))
            setup(dve.tensor_tensor(sp_l[:, :, :], sp_l[:, :, :], sp_u[:, :, :], ALU.add))
            setup(dve.scalar_tensor_tensor(msp[:, :, :], msp[:, :, :], 0.0, sp_l[:, :, :], ALU.max, ALU.add))
            for i in range(HID):
                setup(dve.tensor_tensor(coef[0:HR, :, i], msp[0:HR, :, M1C + i], fth[0:HR, :, F0O], ALU.mult))
                setup(dve.tensor_tensor(coef[HR:P, :, i], msp[HR:P, :, M1 + HID * i], msp[HR:P, :, M0], ALU.mult))
                for j in range(1, HID):
                    setup(dve.tensor_tensor(prod[HR:P, :], msp[HR:P, :, M1 + HID * i + j], msp[HR:P, :, M0 + j],
                                            ALU.mult))
                    setup(dve.tensor_tensor(coef[HR:P, :, i], coef[HR:P, :, i], prod[HR:P, :], ALU.add))
            for i in range(HID):
                mul_add(c1_all[:, :, i], bra[:, :, B1 + i],
                        [(msp[:, :, M1 + HID * i + j], bra[:, :, B0 + j]) for j in range(HID)])
            for i in range(HID):
                mul_add(c2_all[:, :, i], bra[:, :, B2 + i],
                        [(msp[:, :, M2 + HID * i + j], c1_all[:, :, j]) for j in range(HID)])
            mul_add(w_all[:, :, SC_C1], bra[:, :, B1O], [(msp[:, :, M1R + j], bra[:, :, B0 + j]) for j in range(HID)])
            mul_add(w_all[:, :, SC_C2], bra[:, :, B2O], [(msp[:, :, M2R + j], c1_all[:, :, j]) for j in range(HID)])
            mul_add(w_all[:, :, SC_C3], bra[:, :, B3], [(msp[:, :, M3 + j], c2_all[:, :, j]) for j in range(HID)])
            setup(dve.tensor_copy(w_all[:, :, SC_SP0], msp[:, :, M0R]))
            setup(dve.scalar_tensor_tensor(w_all[:, :, SC_BL], msp[:, :, M0R], -0.5, bra[:, :, B0O], ALU.mult, ALU.add))
            setup(dve.scalar_tensor_tensor(w_all[:, :, SC_BU], msp[:, :, M0R], 0.5, bra[:, :, B0O], ALU.mult, ALU.add))
            setup(dve.tensor_copy(w_all[:, :, SC_T1], fth[:, :, F1O]))
            setup(dve.tensor_copy(w_all[:, :, SC_T2], fth[:, :, F2O]))
            setup(dve.tensor_scalar(ncols[:, :], cols_sb[:, :], -1.0, None, ALU.mult))
            setup(dve.tensor_copy(eye16[:, :], eye_sb[:, :]))
            assert steps[0] == SETUP_STEPS, steps[0]

            def groupnorm(b, k):
                base = dve.compute_val(b * 2 * STAT_STEPS + k * STAT_STEPS)
                n = [0]

                def step(ins):
                    n[0] += 1
                    ins.then_inc(stat_step, 1)
                    dve.wait_ge(stat_step, base + n[0])

                dve.bn_aggr(mv[:, 0, :], stats[:, 0, :, :])
                step(dve.bn_aggr(mv[:, 1, :], stats[:, 1, :, :]))
                dve.wait_ge(stat_mm, b * 4 + 2 * k + 1)
                step(dve.tensor_copy(gmean[:, :], ps[0:HALF, 0, 0:2]))
                step(dve.tensor_tensor(tmp_a[:, :], mv[:, :, 0], gmean[:, :], ALU.subtract))
                step(dve.tensor_tensor(tmp_b[:, :], tmp_a[:, :], tmp_a[:, :], ALU.mult))
                step(dve.tensor_tensor(tmp_a[:, :], tmp_b[:, :], mv[:, :, 1], ALU.add))
                dve.wait_ge(stat_mm, b * 4 + 2 * k + 2)
                step(dve.tensor_scalar(gvar[:, :], ps[0:HALF, 1, 0:2], EPS, None, ALU.add))
                dve.wait_ge(stat_std, b * 2 + k + 1)
                step(dve.reciprocal(rstd[:, :], gstd[:, :]))
                step(dve.tensor_tensor(tmp_a[:, :], rstd[:, :], rstd[:, :], ALU.mult))
                step(dve.tensor_tensor(tmp_b[:, :], tmp_a[:, :], gvar[:, :], ALU.mult))
                step(dve.tensor_scalar(tmp_a[:, :], tmp_b[:, :], -0.5, 1.5, ALU.mult, ALU.add))
                step(dve.tensor_tensor(rstd[:, :], rstd[:, :], tmp_a[:, :], ALU.mult))
                assert n[0] == STAT_STEPS
                for h in range(2):
                    dve.tensor_scalar(xn[0:HALF, h, :], x_sb[:, h, :], gmean[:, h:h + 1], rstd[:, h:h + 1],
                                      ALU.subtract, ALU.mult).then_inc(xn_ready, 1)

            def statistics(b, h):
                dve.wait_ge(x_in[h], b * 16 + 16)
                for j in range(BLOCKS):
                    ins = dve.bn_stats(stats[:, h, j, :], x_sb[:, h, j * N:(j + 1) * N])
                ins.then_inc(x_stat, 1)

            def first_norm(b):
                stat_now = dve.compute_val(b * 2 + 2)
                settle(dve)
                dve.wait_ge(x_stat, stat_now)
                groupnorm(b, 0)

            def image(b, last):
                def reduce(base, m):
                    dve.wait_ge(max_mm, base + m + 1)
                    dve.tensor_reduce(mxp[:, m // BLOCKS, m % BLOCKS:m % BLOCKS + 1], ps[:, 4 + bank_of[0] + m % 2, :],
                                      AX_X, ALU.max).then_inc(max_red, 1)

                bank_of = [0]

                def split_max(g, base):
                    st = dve.compute_val(g * MAX_STEPS)
                    n = [0]

                    def step(ins):
                        n[0] += 1
                        ins.then_inc(max_step, 1)
                        dve.wait_ge(max_step, st + n[0])

                    dve.wait_ge(max_red, base + MAXES)
                    step(dve.tensor_reduce(mx[:, :], mxp[:, :, :], AX_X, ALU.max))
                    step(dve.tensor_scalar(negm[:, :], mx[:, :], -1.0, ESHIFT, ALU.mult, ALU.add))
                    step(dve.tensor_scalar(mparts[:, 0, :], negm[:, :], 1.0 / BIG, None, ALU.mult))
                    step(dve.scalar_tensor_tensor(rest[:, :], mparts[:, 0, :], -BIG, negm[:, :], ALU.mult, ALU.add))
                    step(dve.tensor_copy(mparts[:, 1, :], rest[:, :]))
                    step(dve.tensor_tensor(mparts[:, 2, :], rest[:, :], mparts[:, 1, :], ALU.subtract))
                    assert n[0] == MAX_STEPS

                def rows_out(g, bank, first=False):
                    dve.wait_ge(max_turn, g + 1)
                    if not first:
                        dve.wait_ge(max_in, g * 16)
                    dve.tensor_copy(mrows[:, :], ps[0:3 * NT, bank, 0:P // 2].bitcast(F16)).then_inc(max_rows, 1)

                blocks0 = dve.compute_val(b * BLOCKS)
                maxes0 = dve.compute_val(b * BLOCKS * MAXES)
                bank_of[0] = own_banks(0) - 4
                for n in range(4 * BLOCKS):
                    v = n - 2 * BLOCKS
                    w = N if v < 0 else 2 * C
                    col = COL_A2 if n < BLOCKS else COL_A1 if v < 0 else COL_AA
                    s = n % 2
                    dve.wait_ge(proj_act, b * 4 * BLOCKS + n + 1)
                    if v in (0, 1):
                        dve.wait_ge(qk_done, b * 2 * BLOCKS + 2 * BLOCKS - 1 + v)
                    if v >= 2:
                        dve.wait_ge(v_done, b * 2 * BLOCKS + v - 1)
                    dve.scalar_tensor_tensor(p_val[:, s, 0:w], p_neg[:, s, 0:w], ncols[:, col:col + 1],
                                             p_pos[:, s, 0:w], ALU.mult, ALU.add).then_inc(proj_val, 1)
                    if v < 0:
                        dve.wait_ge(proj_val, b * 4 * BLOCKS + n + 1)
                        st = (kst if n < BLOCKS else qst)[:, (n % BLOCKS) * N:(n % BLOCKS + 1) * N]
                        mask = COL_MK if n < BLOCKS else COL_MQ
                        dve.tensor_copy(p_hi[:, s, :], p_val[:, s, :]).then_inc(qk_hi, 1)
                        dve.wait_ge(qk_hi, b * 2 * BLOCKS + n + 1)
                        dve.scalar_tensor_tensor(st, p_hi[:, s, :], cols_sb[:, mask:mask + 1], p_val[:, s, :],
                                                 ALU.mult, ALU.add).then_inc(qk_done, 1)
                    else:
                        for m in first_maxes(v):
                            reduce(maxes0, m)
                        if v == FIRST_SPLIT:
                            split_max(blocks0, maxes0)
                        if v == FIRST_SPLIT + 1:
                            rows_out(blocks0, own_banks(0), True)

                def low(pairs, q):
                    dve.wait_ge(full_ready, pairs + q + 1)
                    dve.tensor_tensor(e_lo[:, q % 4, :], e_32[:, q % 2, :], e_hi[:, q % 4, :],
                                      ALU.subtract).then_inc(lo_ready, 1)

                def denominators(j, bank):
                    dve.wait_ge(summed, b * BLOCKS * PAIRS + j * PAIRS + PAIRS)
                    dve.wait_ge(out_norm, b * BLOCKS + j + START)
                    sums = ps[:, bank:bank + 2, :].rearrange("p k (t n) -> p k t n", t=2)
                    dve.reciprocal(rden[:, :].rearrange("p (k t) -> p k t", k=2), sums[:, :, :, C]
                                   ).then_inc(den_ready, 1)

                def add_half(j, col, h, bank):
                    dve.wait_ge(out_turn, b * 2 * BLOCKS + 2 * j + h + 1 + START)
                    xs = x_sb[:, h, bass.ds(col, N)]
                    dve.tensor_tensor(xs, ps[0:HALF, bank, :], xs, ALU.add).then_inc(x2_ready, 1)
                    dve.wait_ge(x2_ready, b * 2 * BLOCKS + 2 * j + h + 1 + START)
                    dve.bn_stats(stats[:, h, bass.ds(j, 1), :].rearrange("p a n -> p (a n)"), xs).then_inc(x2_stat, 1)

                def body(before, parity, first, last):
                    j = before + (0 if first else 1)
                    pairs = dve.compute_val(b * BLOCKS * PAIRS + j * PAIRS)
                    maxes = dve.compute_val(b * BLOCKS * MAXES + j * MAXES + MAXES)
                    nxt = dve.compute_val(b * BLOCKS + j + 1)
                    col = dve.compute_val(before * N)
                    free = own_banks(1 - parity)
                    bank_of[0] = free - 4
                    for p in range(PAIRS):
                        if p == 0 and not first:
                            denominators(before, free)
                        if p == 12 and not last:
                            rows_out(nxt, free)
                        if p + 1 < PAIRS or not last:
                            low(pairs, p + 1)
                        if not last:
                            for m in range(PER_STEP * p, min(PER_STEP * (p + 1), MAXES)):
                                reduce(maxes, m)
                            if p == 11:
                                split_max(nxt, maxes)
                        if not first and p in (13, 14):
                            add_half(before, col, p - 13, free + 1 - (p - 13))

                low(dve.compute_val(b * BLOCKS * PAIRS), 0)
                body(0, 0, True, False)
                with dve.Fori(0, (BLOCKS - 2) // 2) as jj:
                    body(dve.compute_val(jj * 2), 1, False, False)
                    body(dve.compute_val(jj * 2 + 1), 0, False, False)
                body(BLOCKS - 2, 1, False, True)
                denominators(BLOCKS - 1, own_banks(1))
                for h in range(2):
                    add_half(BLOCKS - 1, (BLOCKS - 1) * N, h, own_banks(0) + 1 - h)
                settle(dve)
                dve.wait_ge(x2_stat, b * 2 * BLOCKS + 2 * BLOCKS)
                groupnorm(b, 1)

                def gate(c, t, dst, slots, col, before, after):
                    bank = 2 * (c % 3)
                    dve.wait_ge(before, b * SLOTS + c + 1)
                    dve.scalar_tensor_tensor(dst[0:HR, c % slots, :, :], t[0:HR, c % 2, :, :],
                                             w_all[0:HR, c // CHUNKS // 2, col:col + 1], ps[0:HR, bank:bank + 2, :],
                                             ALU.mult, ALU.add).then_inc(after, 1)

                def result(u):
                    s = u % 2
                    dve.wait_ge(sig_ready, b * UNITS + u + 1)
                    dve.tensor_tensor(dif, sig[:, 1, :], sig[:, 0, :], ALU.subtract).then_inc(dif_ready, 1)
                    dve.wait_ge(dif_ready, b * UNITS + u + 1)
                    dve.scalar_tensor_tensor(size, dif, -1.0, dif, ALU.mult, ALU.max).then_inc(size_ready, 1)
                    dve.wait_ge(size_ready, b * UNITS + u + 1)
                    dve.wait_ge(x2t_in[s], b * HALF_UNITS * CHUNKS + 16 * CHUNKS * (u // 2 + 1))
                    if u >= 2:
                        dve.wait_ge(stored[s], b * HALF_UNITS + 16 * (u // 2))
                    dve.scalar_tensor_tensor(res[:, s, :], size, 1e-6, x2t[:, s, :], ALU.max,
                                             ALU.add).then_inc(res_ready, 1)

                def side(u, d):
                    s = u % 2
                    if d == 0:
                        dve.wait_ge(x4_in[s], b * HALF_UNITS * 4 + 64 * (u // 2 + 1))
                        if u >= 2:
                            dve.wait_ge(h1_mm, b * SLOTS + CHUNKS * (u - 1))
                    ins = dve.tensor_scalar(t0[HR:P, s, d, :], x4[HR:P, s, :], 0.5, None,
                                            ALU.subtract if d == 0 else ALU.add)
                    if d == 1:
                        ins.then_inc(x_side, 1)

                side(0, 0)
                side(0, 1)
                for s in range(SLOTS + 5):
                    if s < SLOTS:
                        if s >= 2:
                            dve.wait_ge(h2_mm, b * SLOTS + s - 1)
                        gate(s, t1, h1, 2, SC_T1, t1_ready, h1_ready)
                    if 1 <= s <= SLOTS:
                        if s > H2_SLOTS:
                            dve.wait_ge(h3_mm, b * UNITS + (s - 1 - H2_SLOTS) // CHUNKS + 1)
                        gate(s - 1, t2, h2, H2_SLOTS, SC_T2, t2_ready, h2_ready)
                    if s % CHUNKS in (1, 2) and s // CHUNKS + 1 < UNITS:
                        side(s // CHUNKS + 1, s % CHUNKS - 1)
                    if s >= 8 and (s - 8) % CHUNKS == 0 and (s - 8) // CHUNKS < UNITS - 1:
                        result((s - 8) // CHUNKS)
                    if s == SLOTS - 2 and not last:
                        statistics(dve.compute_val(b + 1), 0)
                if not last:
                    statistics(dve.compute_val(b + 1), 1)
                    first_norm(dve.compute_val(b + 1))
                result(UNITS - 1)

            for h in range(2):
                statistics(0, h)
            first_norm(0)
            with dve.Fori(0, B - 1) as b:
                image(b, False)
            image(B - 1, True)

        @block.tensor
        def _(pe):
            pe.wait_ge(consts_in, CONST_DMAS * 16)
            pe.wait_ge(set_gp, 2)
            def averages(b, k):
                pe.wait_ge(stat_step, b * 2 * STAT_STEPS + k * STAT_STEPS + 1)
                pe.matmul(ps[0:HALF, 0, 0:2], g6_sb[:, :], mv[:, :, 0], start=True, stop=True
                          ).then_inc(stat_mm, 1)
                pe.wait_ge(stat_step, b * 2 * STAT_STEPS + k * STAT_STEPS + 5)
                pe.matmul(ps[0:HALF, 1, 0:2], g6_sb[:, :], tmp_a[:, :], start=True, stop=True
                          ).then_inc(stat_mm, 1)

            def image(b, last):
                pe.wait_ge(xn_ready, b * 4 + 2)

                def bank_free(n):
                    if n >= 4:
                        pe.wait_ge(proj_act, b * 4 * BLOCKS + n - 3)

                for n in range(2 * BLOCKS):
                    bank_free(n)
                    which = 1 if n < BLOCKS else 0
                    c0 = (n % BLOCKS) * N
                    for h in range(2):
                        ins = pe.matmul(ps[:, n % 4, :], wqk_sb[:, h, which, :], xn[0:HALF, h, c0:c0 + N],
                                        start=(h == 0), stop=(h == 1))
                    ins.then_inc(proj_mm, 1)

                def max_tile(base, q_col, m, bank, evacuated):
                    if m >= 2:
                        pe.wait_ge(max_red, base + m - 1)
                    elif evacuated is not None:
                        pe.wait_ge(out_norm, evacuated + START)
                    pe.matmul(ps[:, bank + m % 2, :], qst[:, bass.ds(q_col + (m // BLOCKS) * P, P)],
                              kst[:, (m % BLOCKS) * N:(m % BLOCKS + 1) * N], start=True, stop=True
                              ).then_inc(max_mm, 1)

                def turn_max(g, bank):
                    pe.wait_ge(max_step, g * MAX_STEPS + MAX_STEPS)
                    pe.transpose(ps[0:3 * NT, bank, 0:P // 2].bitcast(F16), mparts[:, :, :]
                                 .rearrange("p r t -> p (r t)"), eye16[:, :]).then_inc(max_turn, 1)

                maxes0 = pe.compute_val(b * BLOCKS * MAXES)
                blocks0 = pe.compute_val(b * BLOCKS)
                def value_bank(v):
                    n = 2 * BLOCKS + v
                    bank_free(n)
                    for k in range(2):
                        m = 2 * v + k
                        pe.matmul(ps[:, n % 4, k * C:(k + 1) * C], xn[0:HALF, 0, m * P:(m + 1) * P],
                                  wv_sb[0:HALF, 0, :], start=True, stop=False)
                        ins = pe.matmul(ps[:, n % 4, k * C:(k + 1) * C], xn[:, 1, m * P:(m + 1) * P],
                                        wv_sb[:, 1, :], start=False, stop=True)
                    ins.then_inc(proj_mm, 1)

                value_bank(0)
                value_bank(1)
                for v in range(2 * BLOCKS):
                    if v + 2 < 2 * BLOCKS:
                        value_bank(v + 2)
                    if v == FIRST_MAX:
                        pe.wait_ge(qk_done, b * 2 * BLOCKS + 2 * BLOCKS)
                    if v == FIRST_SPLIT + 1:
                        turn_max(blocks0, own_banks(0))
                    for m in first_maxes(v):
                        max_tile(maxes0, 0, m, own_banks(0), None)

                def turn_out(slot, h, bank):
                    for t in range(NT):
                        ins = pe.transpose(ps[0:HALF, bank, t * P:(t + 1) * P],
                                           o_sb[:, slot, t, h * HALF:(h + 1) * HALF], eye_sb[:, :])
                    ins.then_inc(out_turn, 1)

                def scores(pairs, q_col, q):
                    for i in range(2):
                        m = (2 * q + i) % MT
                        ins = pe.matmul(ps[:, 2 * (q % 2) + i, :], kst[:, m * P:(m + 1) * P],
                                        qst[:, bass.ds(q_col, N)], start=True, stop=True)
                    ins.then_inc(scored, 1)

                def body(before, parity, first, last):
                    j = before + (0 if first else 1)
                    pairs = pe.compute_val(b * BLOCKS * PAIRS + j * PAIRS)
                    maxes = pe.compute_val(b * BLOCKS * MAXES + j * MAXES + MAXES)
                    blocks = pe.compute_val(b * BLOCKS + j)
                    q_col = pe.compute_val(j * N)
                    q_next = pe.compute_val(j * N + N)
                    mine, free = own_banks(parity), own_banks(1 - parity)
                    for p in range(PAIRS):
                        if p == 12 and not last:
                            turn_max(blocks + 1, free)
                        if p + 2 < PAIRS or not last:
                            pe.wait_ge(full_ready, pairs + p + 1)
                            if p + 2 == PAIRS:
                                pe.wait_ge(max_in, blocks * 16 + 32)
                            scores(pairs, q_col if p + 2 < PAIRS else q_next, p + 2)
                        pe.wait_ge(lo_ready, pairs + p + 1)
                        if p == 0 and first:
                            pe.wait_ge(v_done, b * 2 * BLOCKS + 2 * BLOCKS)
                            pe.wait_ge(ones_col, b + 1)
                        if p == 0 and not first:
                            pe.wait_ge(x2_ready, b * 2 * BLOCKS + 2 * before + START)
                        todo = list(range(PER_STEP * p, min(PER_STEP * (p + 1), MAXES))) if not last else []
                        spots = (5, 6, 7) if p == 0 else (2, 5, 7)
                        for i in range(2):
                            m = 2 * p + i
                            for t in range(NT):
                                eh = e_hi[:, p % 4, i * N + t * P:i * N + (t + 1) * P]
                                el = e_lo[:, p % 4, i * N + t * P:i * N + (t + 1) * P]
                                acc = ps[:, mine + t // 2, (t % 2) * 256:(t % 2) * 256 + C + 1]
                                pe.matmul(acc, eh, v_sb[:, m, 0:C + 1], start=(m == 0 and t % 2 == 0), stop=False,
                                          skip_group_check=True)
                                pe.matmul(acc[:, 0:C], eh, v_sb[:, m, VW:VW + C], start=False, stop=False,
                                          skip_group_check=True)
                                ins = pe.matmul(acc, el, v_sb[:, m, 0:C + 1], start=False, stop=(m == MT - 1),
                                                skip_group_check=True)
                                if i == 1 and t == NT - 1:
                                    ins.then_inc(summed, 1)
                                if i * NT + t in spots and todo:
                                    max_tile(maxes, q_next, todo.pop(0), free,
                                             None if first else blocks)
                        if not first and p in (12, 13):
                            if p == 12:
                                pe.wait_ge(out_norm, blocks + START)
                            elif not last:
                                pe.wait_ge(max_rows, blocks + 2)
                            turn_out(1 - parity, p - 12, free + 1 - (p - 12))

                pe.wait_ge(max_in, b * BLOCKS * 16 + 16)
                pe.wait_ge(proj_act, b * 4 * BLOCKS + 4 * BLOCKS)
                pairs0 = pe.compute_val(b * BLOCKS * PAIRS)
                scores(pairs0, 0, 0)
                scores(pairs0, 0, 1)
                body(0, 0, True, False)
                with pe.Fori(0, (BLOCKS - 2) // 2) as jj:
                    body(pe.compute_val(jj * 2), 1, False, False)
                    body(pe.compute_val(jj * 2 + 1), 0, False, False)
                body(BLOCKS - 2, 1, False, True)
                pe.wait_ge(out_norm, b * BLOCKS + BLOCKS + START)
                pe.wait_ge(x2_ready, b * 2 * BLOCKS + 2 * BLOCKS - 2 + START)
                for h in range(2):
                    turn_out(1, h, own_banks(0) + 1 - h)
                averages(b, 1)

                for s in range(SLOTS + 2):
                    if s < SLOTS:
                        u, k = s // CHUNKS, s % CHUNKS
                        if k % 2 == 0:
                            pe.wait_ge(t0_ready, b * (SLOTS // 2) + s // 2 + 1)
                        if k == 0:
                            pe.wait_ge(x_side, b * UNITS + u + 1)
                        if s >= 3:
                            pe.wait_ge(h2_ready, b * SLOTS + s - 2)
                        for d in range(2):
                            ins = pe.matmul(ps[0:HR, 2 * (s % 3) + d, :], w_all[:, u // 2, 0:HR],
                                            t0[:, u % 2, d, k * N:(k + 1) * N], start=True, stop=True)
                        ins.then_inc(h1_mm, 1)
                    if 1 <= s <= SLOTS:
                        c = s - 1
                        pe.wait_ge(h1_ready, b * SLOTS + c + 1)
                        for d in range(2):
                            ins = pe.matmul(ps[0:HR, 2 * (c % 3) + d, :], w_all[0:HR, c // CHUNKS // 2, HR:2 * HR],
                                            h1[0:HR, c % 2, d, :], start=True, stop=True)
                        ins.then_inc(h2_mm, 1)
                    if s >= CHUNKS + 1 and (s - 1) % CHUNKS == 0:
                        u = (s - 1) // CHUNKS - 1
                        pe.wait_ge(h2_ready, b * SLOTS + CHUNKS * (u + 1))
                        if u >= 1:
                            pe.wait_ge(lu_ready, b * UNITS + u)
                        for d in range(2):
                            for k in range(CHUNKS):
                                ins = pe.matmul(ps[k * G:(k + 1) * G, 6 + d, :],
                                                w_all[0:HR, u // 2, 2 * HR:WCOLS],
                                                h2[0:HR, (CHUNKS * u + k) % H2_SLOTS, d, :], start=True, stop=True)
                        ins.then_inc(h3_mm, 1)

                if not last:
                    averages(pe.compute_val(b + 1), 0)

            averages(0, 0)
            with pe.Fori(0, B - 1) as b:
                image(b, False)
            image(B - 1, True)


def layout(inputs):
    import numpy as np
    a = {k: np.asarray(v) for k, v in inputs.items()}
    f = np.float32
    wqk = np.zeros((C, 2, P), f)
    cols = np.zeros((P, NCOLS), f)
    for k in range(P // SUB):
        wqk[:, 0, k * SUB:k * SUB + CR] = a["L0_conv_w1"].T
        wqk[:, 1, k * SUB:k * SUB + CR] = a["L0_conv_w2"].T
        cols[k * SUB:k * SUB + CR, COL_BQ] = a["L0_conv_b1"]
        cols[k * SUB:k * SUB + CR, COL_BK] = a["L0_conv_b2"]
    cols[CR:CR + 3, COL_BK] = (BIG, 1.0, 1.0)
    cols[:, COL_A1], cols[:, COL_A2], cols[:, COL_AA] = a["L0_conv_a1"], a["L0_conv_a2"], a["L0_conv_aa"]
    cols[2 * SUB:, COL_MQ] = -1.0
    cols[SUB:2 * SUB, COL_MK] = cols[3 * SUB:, COL_MK] = -1.0
    wv = np.concatenate([a["L0_conv_wa"].T, a["L0_conv_ba"][None, :]], 0)
    per = C // 32
    g6 = np.kron(np.eye(HALF // per, dtype=f), np.full((per, per), 1.0 / per, f))
    diag = np.tile(np.eye(G, dtype=f), (4, 1))

    def rows(of):
        parts = [of(min(j, HID - 1)).reshape(GROUPS, G, -1).transpose(1, 0, 2) for j in range(4)]
        return np.ascontiguousarray(np.concatenate(parts, 0))

    m0, m1, m2, m3 = (a[f"L1_conv_m{i}"] for i in range(4))
    b0, b1, b2, b3 = (a[f"L1_conv_b{i}"][:, :, 0] for i in range(4))
    f0, f1, f2 = (a[f"L1_conv_f{i}"][:, :, 0] for i in range(3))
    mraw = rows(lambda j: np.concatenate([
        m0[:, :, 0], m1.reshape(C, 9), m2.reshape(C, 9), m3[:, 0, :],
        m1[:, :, j], m2[:, :, j], m3[:, 0, j:j + 1], m0[:, j], m1[:, j, :], m2[:, j, :]], 1))
    fraw = rows(lambda j: np.stack([f0[:, j], f1[:, j], f2[:, j]], 1))
    braw = rows(lambda j: np.concatenate([b0, b1, b2, b3, b0[:, j:j + 1], b1[:, j:j + 1], b2[:, j:j + 1]], 1))
    return {"x": np.ascontiguousarray(a["x"]), "wqk": wqk, "wv": np.ascontiguousarray(wv), "cols": cols, "g6": g6,
            "eye": np.eye(P, dtype=f), "diag": diag, "mraw": mraw, "fraw": fraw, "braw": braw}


def kernel(**inputs):
    import concourse.bacc as bacc
    from concourse.bass_utils import run_bass_kernel_spmd

    nc = bacc.Bacc("TRN2", target_bir_lowering=False, num_devices=1)
    arrays = layout(inputs)
    args = [nc.dram_tensor(f"{name}_dram", a.shape, mybir.dt.from_np(a.dtype), kind="ExternalInput").ap()
            for name, a in arrays.items()]
    out = nc.dram_tensor("out_dram", arrays["x"].shape, F32, kind="ExternalOutput").ap()
    program(nc, *args, out)
    r = run_bass_kernel_spmd(nc, [{f"{name}_dram": a for name, a in arrays.items()}], core_ids=[0])
    return r.results[0]["out_dram"]
```

```python
from contextlib import ExitStack

import concourse.bass as bass
from concourse import mybir

ALU = mybir.AluOpType
ACT = mybir.ActivationFunctionType
F32 = mybir.dt.float32
F16 = mybir.dt.float16
AX_X = mybir.AxisListType.X

B, C, HW = 8, 192, 64 * 64
CR = C // 8
P = 128
HALF = C // 2
N = 512
BLOCKS = HW // N
NT = N // P
MT = HW // P
PAIRS = MT // 2
MAXES = NT * BLOCKS
SUB = 32
VW = C + 2
EPS = 1e-5
LN2 = 0.6931471805599453
ESHIFT = 14 * LN2
BIG = 4096.0
PER_STEP = 3

QK_BANKS = BLOCKS
V_BANKS = PAIRS
BANKS = QK_BANKS + V_BANKS

COL_B, COL_A, COL_AA, COL_M = range(4)
NCOLS = 4
STACK_DMAS = 5
CONST_DMAS = 10

G = 32
GROUPS = C // G
HID = 3
HR = HID * G
CHUNKS = 4
UN = CHUNKS * N
WCOLS = HR + HR + G
SC_SP0, SC_BL, SC_BU, SC_C1, SC_C2, SC_T1, SC_T2, SC_C3 = range(WCOLS, WCOLS + 8)
WROW = WCOLS + 8
UNITS = 2 * GROUPS
SLOTS = UNITS * CHUNKS

M0, M1, M2, M3 = 0, 3, 12, 21
M1C, M2C, M3C = 24, 27, 30
M0R, M1R, M2R = 31, 32, 35
NM = 38
F0O, F1O, F2O = 0, 1, 2
NF = 3
B0, B1, B2, B3, B0O, B1O, B2O = 0, 3, 6, 9, 10, 11, 12
NB = 13

SETUP_STEPS = 9 + 2
COEF_STEPS = 3 * 6 + 9 * 6 + 7
STAT_STEPS = 11
H2_SLOTS = 4
TANH_LEAD = 4
STATS_AT = 36
START = 1
FIRST_PIECES, SECOND_PIECES = 8, 4
MAX_STEPS = 6
FIRST_MAX = 2
FIRST_STEP = 4
FIRST_SPLIT = FIRST_MAX + MAXES // FIRST_STEP


def first_maxes(v):
    start = FIRST_STEP * (v - FIRST_MAX)
    return range(start, start + FIRST_STEP) if FIRST_MAX <= v < FIRST_SPLIT else ()


POOL_VALS = 10
VALS = BANKS - POOL_VALS


def on_pool(n):
    return FIRST_MAX <= n - QK_BANKS < FIRST_MAX + POOL_VALS


def program(nc, x, wqk, wv, cols, g6, eye, diag, mraw, fraw, braw, out):
    x_rows = x.rearrange("b c h w -> (b c) (h w)")
    out_rows = out.rearrange("b c h w -> (b c) (h w)")
    with ExitStack() as ctx:
        def sb(name, shape, dt=F32):
            return ctx.enter_context(nc.sbuf_tensor(name, shape, dt))

        def sem(name):
            return ctx.enter_context(nc.semaphore(name))

        x_sb = sb("x_sb", [HALF, 2, HW])
        xn = sb("xn", [HALF + 1, 2, HW])
        wqk_sb = sb("wqk_sb", [HALF, 2, P])
        wv_sb = sb("wv_sb", [HALF + 1, 2, C])
        cols_sb = sb("cols_sb", [P, NCOLS])
        ncols = sb("ncols", [P, NCOLS])
        g6_sb = sb("g6_sb", [HALF, HALF])
        eye_sb = sb("eye_sb", [P, P])
        eye16 = sb("eye16", [P, P], F16)
        diag_sb = sb("diag_sb", [P, G])
        stats = sb("stats", [HALF, 2, BLOCKS, 6])
        mv = sb("mv", [HALF, 2, 2])
        gmean = sb("gmean", [HALF, 2])
        gvar = sb("gvar", [HALF, 2])
        gstd = sb("gstd", [HALF, 2])
        rstd = sb("rstd", [HALF, 2])
        tmp_a = sb("tmp_a", [HALF, 2])
        tmp_b = sb("tmp_b", [HALF, 2])
        mxp = sb("mxp", [P, NT, BLOCKS])
        mx = sb("mx", [P, NT])
        negm = sb("negm", [P, NT])
        rest = sb("rest", [P, NT])
        mparts = sb("mparts", [P, 3, NT], F16)
        mrows = sb("mrows", [3 * NT, P], F16)
        rden = sb("rden", [P, NT])
        warm = sb("warm", [P, 1])
        w_all = sb("w_all", [P, GROUPS, WROW])
        msp = sb("msp", [P, GROUPS, NM])
        fth = sb("fth", [P, GROUPS, NF])
        bra = sb("bra", [P, GROUPS, NB])
        sp_abs = sb("sp_abs", [P, GROUPS, NM])
        sp_e = sb("sp_e", [P, GROUPS, NM])
        sp_u = sb("sp_u", [P, GROUPS, NM])
        sp_l = sb("sp_l", [P, GROUPS, NM])
        coef = sb("coef", [P, GROUPS, HID])
        c1_all = sb("c1_all", [P, GROUPS, HID])
        c2_all = sb("c2_all", [P, GROUPS, HID])
        prod = sb("prod", [P, GROUPS])

        arena = sb("arena", [P, 30720])
        place = [0]

        def take(words):
            place[0] += words
            return arena[:, place[0] - words:place[0]]

        kst = take(HW // 2).bitcast(F16)
        qst = take(HW // 2).bitcast(F16)
        v_sb = take(MT * (VW + C) // 2).bitcast(F16).rearrange("p (m n) -> p m n", m=MT)
        e_hi = take(4 * N).bitcast(F16).rearrange("p (s n) -> p s n", s=4)
        e_lo = take(4 * N).bitcast(F16).rearrange("p (s n) -> p s n", s=4)
        e_32 = take(2 * 2 * N).rearrange("p (s n) -> p s n", s=2)
        kq = arena[:, place[0] - HW // 2:place[0]].bitcast(F16)
        o_sb = take(2 * NT * C).rearrange("p (s t n) -> p s t n", s=2, t=NT)
        p_pos = take(2 * N).rearrange("p (s n) -> p s n", s=2)
        p_neg = take(2 * N).rearrange("p (s n) -> p s n", s=2)
        p_val = take(2 * N).rearrange("p (s n) -> p s n", s=2)
        first_end, place[0] = place[0], 0
        x4 = take(2 * UN).rearrange("p (s n) -> p s n", s=2)
        t0 = take(2 * 2 * UN).rearrange("p (s d n) -> p s d n", s=2, d=2)
        t1 = take(2 * 2 * N).rearrange("p (s d n) -> p s d n", s=2, d=2)
        t2 = take(2 * 2 * N).rearrange("p (s d n) -> p s d n", s=2, d=2)
        h1 = take(2 * 2 * N).rearrange("p (s d n) -> p s d n", s=2, d=2)
        h2 = take(H2_SLOTS * 2 * N).rearrange("p (s d n) -> p s d n", s=H2_SLOTS, d=2)
        assert first_end <= place[0]
        lu = take(2 * 2 * N).rearrange("p (s d n) -> p s d n", s=2, d=2)
        lu_sum = take(N)
        lu_sign = take(N)
        signed = take(2 * N).rearrange("p (d n) -> p d n", d=2)
        sig = take(2 * N).rearrange("p (d n) -> p d n", d=2)
        dif = take(N)
        res = take(2 * N).rearrange("p (s n) -> p s n", s=2)
        x2t = take(3 * N).rearrange("p (s n) -> p s n", s=3)

        ps = ctx.enter_context(nc.psum_tensor("ps", [P, 8, N], F32))

        def own_banks(g):
            return 4 + 2 * (g % 2)

        consts_in = sem("consts_in")
        set_step = sem("set_step")
        coef_step = sem("coef_step")
        set_act = sem("set_act")
        set_gp = sem("set_gp")
        ones_col = sem("ones_col")
        x_in = [sem(f"x_in{h}") for h in range(2)]
        x_stat = sem("x_stat")
        stat_step = sem("stat_step")
        stat_mm = sem("stat_mm")
        stat_std = sem("stat_std")
        xn_ready = sem("xn_ready")
        proj_mm = sem("proj_mm")
        proj_act = sem("proj_act")
        neg_ready = sem("neg_ready")
        proj_val = sem("proj_val")
        pool_val = sem("pool_val")
        qk_hi = sem("qk_hi")
        qk_done = sem("qk_done")
        stacks_in = [sem(f"stacks_in{i}") for i in range(BLOCKS // 2)]
        v_hi = sem("v_hi")
        v_done = sem("v_done")
        max_mm = sem("max_mm")
        max_red = sem("max_red")
        max_step = sem("max_step")
        max_turn = sem("max_turn")
        max_rows = sem("max_rows")
        max_in = sem("max_in")
        scored = sem("scored")
        full_ready = sem("full_ready")
        lo_ready = sem("lo_ready")
        summed = sem("summed")
        den_ready = sem("den_ready")
        out_norm = sem("out_norm")
        out_turn = sem("out_turn")
        x2_ready = sem("x2_ready")
        x2_stat = sem("x2_stat")
        x4_in = [sem(f"x4_in{s}") for s in range(2)]
        x2t_in = [sem(f"x2t_in{s}") for s in range(3)]
        x_side = sem("x_side")
        t0_ready = sem("t0_ready")
        h1_mm = sem("h1_mm")
        t1_ready = sem("t1_ready")
        h1_ready = sem("h1_ready")
        h2_mm = sem("h2_mm")
        t2_ready = sem("t2_ready")
        h2_ready = sem("h2_ready")
        h3_mm = sem("h3_mm")
        lu_ready = sem("lu_ready")
        sum_ready = sem("sum_ready")
        sign_ready = sem("sign_ready")
        signed_ready = sem("signed_ready")
        sig_ready = sem("sig_ready")
        dif_ready = sem("dif_ready")
        size_ready = sem("size_ready")
        res_ready = sem("res_ready")
        stored = [sem(f"stored{s}") for s in range(2)]

        HALF_UNITS, THIRD_UNITS = UNITS // 2 * 16, UNITS // 3 * 16

        def settle(eng):
            eng.wait_ge(consts_in, CONST_DMAS * 16)

        block = ctx.enter_context(nc.Block())

        @block.sync
        def _(sp):
            for h in range(2):
                sp.dma_start(x_sb[:, h, :], x_rows[h * HALF:(h + 1) * HALF, :]).then_inc(x_in[h], 16)
            for dst, src in ((msp[:, :, :], mraw), (fth[:, :, :], fraw), (g6_sb[:, :], g6),
                             (wqk_sb[:, :, :], wqk.rearrange("(h p) n -> p h n", h=2)), (cols_sb[:, :], cols),
                             (wv_sb[0:HALF, :, :], wv[0:C, :].rearrange("(h p) n -> p h n", h=2)),
                             (wv_sb[HALF:HALF + 1, 1, :], wv[C:C + 1, :]),
                             (eye_sb[:, :], eye), (diag_sb[:, :], diag), (bra[:, :, :], braw)):
                sp.dma_start(dst, src).then_inc(consts_in, 16)

            def image(b, row, last):
                for j in range(0, BLOCKS, 2):
                    sp.wait_ge(qk_done, b * QK_BANKS + j + 2)
                    for stack, to, start, rows in ((kst, 0, 0, 2), (qst, 2, 2, 2), (kst, 2, 0, 2), (qst, 0, 3, 1),
                                                   (qst, 1, 2, 1)):
                        sp.dma_start(stack[to * SUB:(to + rows) * SUB, j * N:(j + 2) * N],
                                     kq[start * SUB:(start + rows) * SUB, j * N:(j + 2) * N]
                                     ).then_inc(stacks_in[j // 2], 16)
                sp.wait_ge(max_rows, b * BLOCKS + 1)
                sp.dma_start(qst[CR:CR + 3, 0:N].rearrange("r (t n) -> r t n", t=NT),
                             mrows[:, :]).then_inc(max_in, 16)
                with sp.Fori(1, BLOCKS) as j:
                    col = sp.compute_val(j * N)
                    sp.wait_ge(max_rows, b * BLOCKS + j + 1)
                    sp.dma_start(qst[CR:CR + 3, bass.ds(col, N)].rearrange("r (t n) -> r t n", t=NT),
                                 mrows[:, :]).then_inc(max_in, 16)
                for u in range(UNITS):
                    s, half = u % 2, u // (UNITS // 2)
                    c0 = (u // 2) * G - half * HALF
                    if u % (UNITS // 2) < 2:
                        sp.wait_ge(xn_ready, b * (FIRST_PIECES + SECOND_PIECES) + FIRST_PIECES + 1 + 2 * half + s)
                    if u >= 2:
                        tanh_read = sp.compute_val(b * SLOTS + (u - 1) * CHUNKS)
                        side_read = sp.compute_val(b * UNITS + u - 1)
                        settle(sp)
                        sp.wait_ge(t0_ready, tanh_read)
                        sp.wait_ge(x_side, side_read)
                    for k in range(4):
                        sp.dma_start(x4[k * G:(k + 1) * G, s, :], xn[c0:c0 + G, half, s * UN:(s + 1) * UN]
                                     ).then_inc(x4_in[s], 16)
                    if u >= 3:
                        store(b, row, u - 3)
                    load_x2(b, u)
                    if u == UNITS // 2 + 1 and not last:
                        next_x(b, row, 0)
                if not last:
                    next_x(b, row, 1)
                for u in range(UNITS - 3, UNITS):
                    store(b, row, u)

            def load_x2(b, u):
                s, half = u % 2, u // (UNITS // 2)
                c0 = (u // 2) * G - half * HALF
                for k in range(CHUNKS):
                    sp.dma_start(x2t[k * G:(k + 1) * G, u % 3, :],
                                 x_sb[c0:c0 + G, half, s * UN + k * N:s * UN + (k + 1) * N]
                                 ).then_inc(x2t_in[u % 3], 16)

            def next_x(b, row, h):
                come = sp.compute_val(b * THIRD_UNITS * CHUNKS + (h + 1) * THIRD_UNITS // 2 * CHUNKS)
                settle(sp)
                for s in range(3):
                    sp.wait_ge(x2t_in[s], come)
                sp.dma_start(x_sb[:, h, :], x_rows[bass.ds(row + (2 + h) * HALF, HALF), :]).then_inc(x_in[h], 16)

            def store(b, row, u):
                sp.wait_ge(res_ready, b * UNITS + u + 1)
                sp.dma_start(out_rows[bass.ds(row + (u // 2) * G, G), (u % 2) * UN:(u % 2 + 1) * UN]
                             .rearrange("c (k n) -> k c n", k=CHUNKS), res[:, u % 2, :]).then_inc(stored[u % 2], 16)

            with sp.Fori(0, B - 1) as b:
                image(b, sp.compute_val(b * C), False)
            image(B - 1, (B - 1) * C, True)
            for s in range(2):
                sp.wait_ge(stored[s], B * HALF_UNITS)

        @block.gpsimd
        def _(pool):
            for counted in (out_norm, out_turn, x2_ready):
                pool.sem_inc(counted, START)
            pool.memset(xn[HALF:HALF + 1, :, :], 1.0).then_inc(set_gp, 1)
            steps = [0]

            def setup(ins):
                steps[0] += 1
                ins.then_inc(coef_step, 1)
                pool.wait_ge(coef_step, steps[0])

            def mul_add(acc, start, factors):
                for n, (a, c) in enumerate(factors):
                    setup(pool.tensor_tensor(prod[:, :], a, c, ALU.mult))
                    setup(pool.tensor_tensor(acc, start if n == 0 else acc, prod[:, :], ALU.add))

            pool.wait_ge(set_gp, 1)
            pool.wait_ge(set_step, SETUP_STEPS)
            for i in range(HID):
                setup(pool.tensor_tensor(coef[0:HR, :, i], msp[0:HR, :, M1C + i], fth[0:HR, :, F0O], ALU.mult))
                setup(pool.tensor_tensor(coef[HR:P, :, i], msp[HR:P, :, M1 + HID * i], msp[HR:P, :, M0], ALU.mult))
                for j in range(1, HID):
                    setup(pool.tensor_tensor(prod[HR:P, :], msp[HR:P, :, M1 + HID * i + j], msp[HR:P, :, M0 + j],
                                            ALU.mult))
                    setup(pool.tensor_tensor(coef[HR:P, :, i], coef[HR:P, :, i], prod[HR:P, :], ALU.add))
            for i in range(HID):
                mul_add(c1_all[:, :, i], bra[:, :, B1 + i],
                        [(msp[:, :, M1 + HID * i + j], bra[:, :, B0 + j]) for j in range(HID)])
            for i in range(HID):
                mul_add(c2_all[:, :, i], bra[:, :, B2 + i],
                        [(msp[:, :, M2 + HID * i + j], c1_all[:, :, j]) for j in range(HID)])
            mul_add(w_all[:, :, SC_C1], bra[:, :, B1O], [(msp[:, :, M1R + j], bra[:, :, B0 + j]) for j in range(HID)])
            mul_add(w_all[:, :, SC_C2], bra[:, :, B2O], [(msp[:, :, M2R + j], c1_all[:, :, j]) for j in range(HID)])
            mul_add(w_all[:, :, SC_C3], bra[:, :, B3], [(msp[:, :, M3 + j], c2_all[:, :, j]) for j in range(HID)])
            setup(pool.tensor_copy(w_all[:, :, SC_SP0], msp[:, :, M0R]))
            for col, shift in ((SC_BL, -0.5), (SC_BU, 0.5)):
                setup(pool.tensor_scalar(prod[:, :], msp[:, :, M0R], shift, None, ALU.mult))
                setup(pool.tensor_tensor(w_all[:, :, col], prod[:, :], bra[:, :, B0O], ALU.add))
            setup(pool.tensor_copy(w_all[:, :, SC_T1], fth[:, :, F1O]))
            setup(pool.tensor_copy(w_all[:, :, SC_T2], fth[:, :, F2O]))
            assert steps[0] == COEF_STEPS, steps[0]
            for g in range(GROUPS):
                for i in range(HID):
                    pool.tensor_scalar(w_all[:, g, i * G:(i + 1) * G], diag_sb[:, :], coef[:, g, i:i + 1], None,
                                       ALU.mult)
                    pool.tensor_scalar(w_all[0:HR, g, HR + i * G:HR + (i + 1) * G], diag_sb[0:HR, :],
                                       msp[0:HR, g, M2C + i:M2C + i + 1], None, ALU.mult)
                ins = pool.tensor_scalar(w_all[0:HR, g, 2 * HR:WCOLS], diag_sb[0:HR, :],
                                         msp[0:HR, g, M3C:M3C + 1], None, ALU.mult)
            ins.then_inc(set_gp, 1)
            with pool.Fori(0, B) as b:
                def add_prelu(n):
                    s = n % 2
                    pool.wait_ge(proj_act, b * BANKS + n + 1)
                    pool.wait_ge(v_done, b * V_BANKS + n - QK_BANKS - 1)
                    pool.tensor_tensor(p_val[:, s, 0:2 * C], p_pos[:, s, 0:2 * C], p_neg[:, s, 0:2 * C],
                                       ALU.add).then_inc(pool_val, 1)

                pool.memset(v_sb[:, :, C:VW], 1.0).then_inc(ones_col, 1)
                for n in range(V_BANKS):
                    if n == FIRST_MAX:
                        add_prelu(QK_BANKS + n)
                    if FIRST_MAX <= n < FIRST_MAX + POOL_VALS - 1:
                        add_prelu(QK_BANKS + n + 1)
                    pool.wait_ge(v_hi, b * V_BANKS + n + 1)
                    pool.tensor_tensor(v_sb[:, 2 * n:2 * n + 2, VW:VW + C],
                                       p_val[:, n % 2, 0:2 * C].rearrange("p (k n) -> p k n", k=2),
                                       v_sb[:, 2 * n:2 * n + 2, 0:C], ALU.subtract).then_inc(v_done, 1)

                def tail(u):
                    s = u % 2
                    pool.wait_ge(lu_ready, b * UNITS + u + 1)
                    if u >= 1:
                        pool.wait_ge(sign_ready, b * UNITS + u)
                    pool.tensor_tensor(lu_sum, lu[:, s, 0, :], lu[:, s, 1, :], ALU.add).then_inc(sum_ready, 1)
                    pool.wait_ge(sign_ready, b * UNITS + u + 1)
                    if u >= 1:
                        pool.wait_ge(sig_ready, b * UNITS + u)
                    pool.tensor_tensor(signed[:, 0, :], lu[:, s, 0, :], lu_sign, ALU.mult)
                    pool.tensor_tensor(signed[:, 1, :], lu[:, s, 1, :], lu_sign, ALU.mult).then_inc(signed_ready, 1)

                for u in range(UNITS):
                    tail(u)

        @block.scalar
        def _(act):
            act.wait_ge(consts_in, CONST_DMAS * 16)
            act.activation(fth[:, :, :], fth[:, :, :], ACT.Tanh).then_inc(set_act, 1)
            act.wait_ge(set_step, 1)
            act.activation(sp_e[:, :, :], sp_abs[:, :, :], ACT.Exp, scale=-1.0).then_inc(set_act, 1)
            act.wait_ge(set_step, 2)
            act.activation(sp_l[:, :, :], sp_u[:, :, :], ACT.Ln).then_inc(set_act, 1)
            act.wait_ge(set_step, SETUP_STEPS)

            def deviation(b, k):
                act.wait_ge(stat_step, b * 2 * STAT_STEPS + k * STAT_STEPS + 6)
                act.activation(gstd[:, :], gvar[:, :], ACT.Sqrt).then_inc(stat_std, 1)

            def image(b, last):
                def val_added(n):
                    if on_pool(n):
                        act.wait_ge(pool_val, b * POOL_VALS + n - QK_BANKS - FIRST_MAX + 1)
                    else:
                        before = n if n - QK_BANKS < FIRST_MAX else n - POOL_VALS
                        act.wait_ge(proj_val, b * VALS + before + 1)

                for n in range(QK_BANKS):
                    act.wait_ge(proj_mm, b * BANKS + n + 1)
                    if n >= 2:
                        val_added(n - 2)
                    act.activation(p_pos[:, n % 2, :], ps[:, n % 4, :], ACT.Relu, bias=cols_sb[:, COL_B:COL_B + 1])
                    act.activation(p_neg[:, n % 2, :], ps[:, n % 4, :], ACT.Relu, bias=ncols[:, COL_B:COL_B + 1],
                                   scale=-1.0).then_inc(proj_act, 1)
                for v in range(V_BANKS + 1):
                    n = QK_BANKS + v
                    pos, neg = p_pos[:, n % 2, 0:2 * C], p_neg[:, n % 2, 0:2 * C]
                    if v < V_BANKS:
                        act.wait_ge(proj_mm, b * BANKS + n + 1)
                        val_added(n - 2)
                        if not on_pool(n):
                            act.activation(pos, ps[:, n % 4, 0:2 * C], ACT.Relu)
                            act.activation(neg, ps[:, n % 4, 0:2 * C], ACT.Relu, scale=-1.0).then_inc(proj_act, 1)
                        else:
                            act.activation(neg, ps[:, n % 4, 0:2 * C], ACT.Relu, scale=-1.0).then_inc(neg_ready, 1)
                            act.activation(pos, ps[:, n % 4, 0:2 * C], ACT.Relu)
                            act.wait_ge(neg_ready, b * POOL_VALS + v - FIRST_MAX + 1)
                            act.activation(neg, neg, ACT.Copy, scale=ncols[:, COL_AA:COL_AA + 1]
                                           ).then_inc(proj_act, 1)
                    if v >= 1:
                        val_added(n - 1)
                        act.activation(v_sb[:, 2 * v - 2:2 * v, 0:C],
                                       p_val[:, (n - 1) % 2, 0:2 * C].rearrange("p (k n) -> p k n", k=2),
                                       ACT.Copy).then_inc(v_hi, 1)

                def exps(pairs, q):
                    sc = ps[:, 2 * (q % 2):2 * (q % 2) + 2, :]
                    act.wait_ge(scored, pairs + q + 1)
                    if q >= 4:
                        act.wait_ge(summed, pairs + q - 3)
                    act.activation(e_hi[:, q % 4, :].rearrange("p (k n) -> p k n", k=2), sc, ACT.Exp)
                    if q >= 2:
                        act.wait_ge(lo_ready, pairs + q - 1)
                    act.activation(e_32[:, q % 2, :].rearrange("p (k n) -> p k n", k=2), sc,
                                   ACT.Exp).then_inc(full_ready, 1)

                def normalise(b, j, slot):
                    act.wait_ge(den_ready, b * BLOCKS + j + 1)
                    act.wait_ge(out_turn, b * 2 * BLOCKS + 2 * j + START)
                    for t in range(NT):
                        ins = act.activation(o_sb[:, slot, t, :],
                                             ps[:, own_banks(slot) + t // 2, (t % 2) * 256:(t % 2) * 256 + C],
                                             ACT.Copy, scale=rden[:, t:t + 1])
                    ins.then_inc(out_norm, 1)

                def body(before, parity, first, last):
                    pairs = act.compute_val(b * BLOCKS * PAIRS + before * PAIRS)
                    for p in range(PAIRS):
                        if p == 0 and not first:
                            normalise(b, before, 1 - parity)
                        if p + 2 < PAIRS or not last:
                            exps(pairs, (0 if first else PAIRS) + p + 2)

                pairs0 = act.compute_val(b * BLOCKS * PAIRS)
                exps(pairs0, 0)
                exps(pairs0, 1)
                body(0, 0, True, False)
                with act.Fori(0, (BLOCKS - 2) // 2) as jj:
                    body(act.compute_val(jj * 2), 1, False, False)
                    body(act.compute_val(jj * 2 + 1), 0, False, False)
                body(BLOCKS - 2, 1, False, True)
                normalise(b, BLOCKS - 1, 1)
                deviation(b, 1)
                act.activation(warm[:, :], rden[:, 0:1], ACT.Sigmoid)

                def first_tanh(c, d):
                    u, k = c // CHUNKS, c % CHUNKS
                    s, g = u % 2, u // 2
                    if k == 0 and d == 0:
                        act.wait_ge(x4_in[s], b * HALF_UNITS * 4 + 64 * (u // 2 + 1))
                        if u >= 2:
                            act.wait_ge(h1_mm, b * SLOTS + CHUNKS * (u - 1))
                    col = SC_BL if d == 0 else SC_BU
                    act.activation(t0[0:HR, s, d, k * N:(k + 2) * N], x4[0:HR, s, k * N:(k + 2) * N],
                                   ACT.Tanh, bias=w_all[0:HR, g, col:col + 1],
                                   scale=w_all[0:HR, g, SC_SP0:SC_SP0 + 1]).then_inc(t0_ready, 1)

                def tanh(c, dst, bank, col, before, after):
                    g = c // CHUNKS // 2
                    act.wait_ge(before, b * SLOTS + c + 1)
                    act.activation(dst[0:HR, c % 2, :, :], ps[0:HR, bank:bank + 2, :], ACT.Tanh,
                                   bias=w_all[0:HR, g, col:col + 1]).then_inc(after, 1)

                def logits(u):
                    act.wait_ge(h3_mm, b * UNITS + u + 1)
                    if u >= 2:
                        act.wait_ge(signed_ready, b * UNITS + u - 1)
                    act.activation(lu[:, u % 2, :, :], ps[:, 6:8, :], ACT.Identity,
                                   bias=w_all[:, u // 2, SC_C3:SC_C3 + 1]).then_inc(lu_ready, 1)

                def sign(u):
                    act.wait_ge(sum_ready, b * UNITS + u + 1)
                    if u >= 1:
                        act.wait_ge(signed_ready, b * UNITS + u)
                    act.activation(lu_sign, lu_sum, ACT.Sign).then_inc(sign_ready, 1)

                def sigmoid(u):
                    act.wait_ge(signed_ready, b * UNITS + u + 1)
                    if u >= 1:
                        act.wait_ge(dif_ready, b * UNITS + u)
                    act.activation(sig[:, :, :], signed[:, :, :], ACT.Sigmoid, scale=-1.0).then_inc(sig_ready, 1)

                act.wait_ge(coef_step, COEF_STEPS)
                for c in range(0, TANH_LEAD, 2):
                    for d in range(2):
                        first_tanh(c, d)
                for s in range(SLOTS + 6):
                    if s < SLOTS:
                        tanh(s, t1, 2 * (s % 3), SC_C1, h1_mm, t1_ready)
                    if 1 <= s <= SLOTS:
                        tanh(s - 1, t2, 2 * ((s - 1) % 3), SC_C2, h2_mm, t2_ready)
                    if s - s % 2 + TANH_LEAD < SLOTS:
                        first_tanh(s - s % 2 + TANH_LEAD, s % 2)
                    u = (s - 5) // CHUNKS
                    if s >= 5 and u < UNITS:
                        if (s - 5) % CHUNKS == 0:
                            logits(u)
                        if (s - 5) % CHUNKS == 1:
                            sign(u)
                        if (s - 5) % CHUNKS == 2:
                            if u == UNITS - 1 and not last:
                                deviation(act.compute_val(b + 1), 0)
                            sigmoid(u)

            deviation(0, 0)
            with act.Fori(0, B - 1) as b:
                image(b, False)
            image(B - 1, True)

        @block.vector
        def _(dve):
            steps = [0]

            def setup(ins):
                steps[0] += 1
                ins.then_inc(set_step, 1)
                dve.wait_ge(set_step, steps[0])

            def statistics(b, h, j):
                if j == 0:
                    dve.wait_ge(x_in[h], b * 16 + 16)
                ins = dve.bn_stats(stats[:, h, j, :], x_sb[:, h, j * N:(j + 1) * N])
                if j == BLOCKS - 1:
                    ins.then_inc(x_stat, 1)

            for j in range(BLOCKS):
                statistics(0, 0, j)
            dve.wait_ge(consts_in, CONST_DMAS * 16)
            setup(dve.scalar_tensor_tensor(sp_abs[:, :, :], msp[:, :, :], -1.0, msp[:, :, :], ALU.mult, ALU.max))
            dve.wait_ge(set_act, 2)
            setup(dve.tensor_scalar(sp_u[:, :, :], sp_e[:, :, :], 1.0, None, ALU.add))
            dve.wait_ge(set_act, 3)
            setup(dve.tensor_scalar(sp_abs[:, :, :], sp_u[:, :, :], 1.0, 1e-30, ALU.subtract, ALU.max))
            setup(dve.reciprocal(sp_abs[:, :, :], sp_abs[:, :, :]))
            setup(dve.tensor_tensor(sp_abs[:, :, :], sp_abs[:, :, :], sp_e[:, :, :], ALU.mult))
            setup(dve.tensor_tensor(sp_l[:, :, :], sp_l[:, :, :], sp_abs[:, :, :], ALU.mult))
            setup(dve.scalar_tensor_tensor(sp_u[:, :, :], sp_u[:, :, :], 1.0, sp_e[:, :, :], ALU.is_equal, ALU.mult))
            setup(dve.tensor_tensor(sp_l[:, :, :], sp_l[:, :, :], sp_u[:, :, :], ALU.add))
            setup(dve.scalar_tensor_tensor(msp[:, :, :], msp[:, :, :], 0.0, sp_l[:, :, :], ALU.max, ALU.add))
            setup(dve.tensor_scalar(ncols[:, :], cols_sb[:, :], -1.0, None, ALU.mult))
            setup(dve.tensor_copy(eye16[:, :], eye_sb[:, :]))
            assert steps[0] == SETUP_STEPS, steps[0]

            def groupnorm(b, k):
                base = dve.compute_val(b * 2 * STAT_STEPS + k * STAT_STEPS)
                n = [0]

                def step(ins):
                    n[0] += 1
                    ins.then_inc(stat_step, 1)
                    dve.wait_ge(stat_step, base + n[0])

                dve.bn_aggr(mv[:, 0, :], stats[:, 0, :, :])
                step(dve.bn_aggr(mv[:, 1, :], stats[:, 1, :, :]))
                dve.wait_ge(stat_mm, b * 4 + 2 * k + 1)
                step(dve.tensor_copy(gmean[:, :], ps[0:HALF, 0, 0:2]))
                step(dve.tensor_tensor(tmp_a[:, :], mv[:, :, 0], gmean[:, :], ALU.subtract))
                step(dve.tensor_tensor(tmp_b[:, :], tmp_a[:, :], tmp_a[:, :], ALU.mult))
                step(dve.tensor_tensor(tmp_a[:, :], tmp_b[:, :], mv[:, :, 1], ALU.add))
                dve.wait_ge(stat_mm, b * 4 + 2 * k + 2)
                step(dve.tensor_scalar(gvar[:, :], ps[0:HALF, 1, 0:2], EPS, None, ALU.add))
                dve.wait_ge(stat_std, b * 2 + k + 1)
                step(dve.reciprocal(rstd[:, :], gstd[:, :]))
                step(dve.tensor_tensor(tmp_a[:, :], rstd[:, :], rstd[:, :], ALU.mult))
                step(dve.tensor_tensor(tmp_b[:, :], tmp_a[:, :], gvar[:, :], ALU.mult))
                step(dve.tensor_scalar(tmp_a[:, :], tmp_b[:, :], -0.5, 1.5, ALU.mult, ALU.add))
                step(dve.tensor_tensor(rstd[:, :], rstd[:, :], tmp_a[:, :], ALU.mult))
                assert n[0] == STAT_STEPS
                pieces = FIRST_PIECES if k == 0 else SECOND_PIECES
                w = 2 * HW // pieces
                for n in range(pieces):
                    h, c = (n % 2, n // 2) if k == 0 else (n // 2, n % 2)
                    dve.tensor_scalar(xn[0:HALF, h, c * w:(c + 1) * w], x_sb[:, h, c * w:(c + 1) * w],
                                      gmean[:, h:h + 1], rstd[:, h:h + 1], ALU.subtract, ALU.mult
                                      ).then_inc(xn_ready, 1)

            def first_norm(b):
                stat_now = dve.compute_val(b * 2 + 2)
                settle(dve)
                dve.wait_ge(x_stat, stat_now)
                groupnorm(b, 0)

            def image(b, last):
                def reduce(base, m, bank):
                    dve.wait_ge(max_mm, base + m + 1)
                    dve.tensor_reduce(mxp[:, m // BLOCKS, m % BLOCKS:m % BLOCKS + 1], ps[:, bank + m % 2, :],
                                      AX_X, ALU.max).then_inc(max_red, 1)

                def split_max(g, base):
                    st = dve.compute_val(g * MAX_STEPS)
                    n = [0]

                    def step(ins):
                        n[0] += 1
                        ins.then_inc(max_step, 1)
                        dve.wait_ge(max_step, st + n[0])

                    dve.wait_ge(max_red, base + MAXES)
                    step(dve.tensor_reduce(mx[:, :], mxp[:, :, :], AX_X, ALU.max))
                    step(dve.tensor_scalar(negm[:, :], mx[:, :], -1.0, ESHIFT, ALU.mult, ALU.add))
                    step(dve.tensor_scalar(mparts[:, 0, :], negm[:, :], 1.0 / BIG, None, ALU.mult))
                    step(dve.scalar_tensor_tensor(rest[:, :], mparts[:, 0, :], -BIG, negm[:, :], ALU.mult, ALU.add))
                    step(dve.tensor_copy(mparts[:, 1, :], rest[:, :]))
                    step(dve.tensor_tensor(mparts[:, 2, :], rest[:, :], mparts[:, 1, :], ALU.subtract))
                    assert n[0] == MAX_STEPS

                def rows_out(g, bank, first=False):
                    dve.wait_ge(max_turn, g + 1)
                    if not first:
                        dve.wait_ge(max_in, g * 16)
                    dve.tensor_copy(mrows[:, :], ps[0:3 * NT, bank, 0:P // 2].bitcast(F16)).then_inc(max_rows, 1)

                blocks0 = dve.compute_val(b * BLOCKS)
                maxes0 = dve.compute_val(b * BLOCKS * MAXES)
                for n in range(BANKS):
                    v = n - QK_BANKS
                    w = N if v < 0 else 2 * C
                    col = COL_A if v < 0 else COL_AA
                    s = n % 2
                    if not on_pool(n):
                        dve.wait_ge(proj_act, b * BANKS + n + 1)
                        if v in (0, 1):
                            dve.wait_ge(qk_done, b * QK_BANKS + QK_BANKS - 1 + v)
                        if v >= 2:
                            dve.wait_ge(v_done, b * V_BANKS + v - 1)
                        dve.scalar_tensor_tensor(p_val[:, s, 0:w], p_neg[:, s, 0:w], ncols[:, col:col + 1],
                                                 p_pos[:, s, 0:w], ALU.mult, ALU.add).then_inc(proj_val, 1)
                    if v < 0:
                        dve.wait_ge(proj_val, b * VALS + n + 1)
                        parts = kq[:, n * N:(n + 1) * N]
                        dve.tensor_copy(parts, p_val[:, s, :]).then_inc(qk_hi, 1)
                        dve.wait_ge(qk_hi, b * QK_BANKS + n + 1)
                        dve.scalar_tensor_tensor(parts, parts, cols_sb[:, COL_M:COL_M + 1], p_val[:, s, :],
                                                 ALU.mult, ALU.add).then_inc(qk_done, 1)
                    else:
                        for m in first_maxes(v)[::2]:
                            dve.wait_ge(max_mm, maxes0 + m + 2)
                            dve.tensor_reduce(mxp[:, m // BLOCKS, m % BLOCKS:m % BLOCKS + 2],
                                              ps[:, 4 + m % 4:6 + m % 4, :], AX_X, ALU.max).then_inc(max_red, 2)
                        if v == FIRST_SPLIT:
                            split_max(blocks0, maxes0)
                        if v == FIRST_SPLIT + 1:
                            rows_out(blocks0, own_banks(0), True)

                def low(pairs, q):
                    dve.wait_ge(full_ready, pairs + q + 1)
                    dve.tensor_tensor(e_lo[:, q % 4, :], e_32[:, q % 2, :], e_hi[:, q % 4, :],
                                      ALU.subtract).then_inc(lo_ready, 1)

                def denominators(j, bank):
                    dve.wait_ge(summed, b * BLOCKS * PAIRS + j * PAIRS + PAIRS)
                    dve.wait_ge(out_norm, b * BLOCKS + j + START)
                    sums = ps[:, bank:bank + 2, :].rearrange("p k (t n) -> p k t n", t=2)
                    dve.reciprocal(rden[:, :].rearrange("p (k t) -> p k t", k=2), sums[:, :, :, C]
                                   ).then_inc(den_ready, 1)

                def add_half(j, col, h, bank):
                    dve.wait_ge(out_turn, b * 2 * BLOCKS + 2 * j + h + 1 + START)
                    xs = x_sb[:, h, bass.ds(col, N)]
                    dve.tensor_tensor(xs, ps[0:HALF, bank, :], xs, ALU.add).then_inc(x2_ready, 1)
                    dve.wait_ge(x2_ready, b * 2 * BLOCKS + 2 * j + h + 1 + START)
                    dve.bn_stats(stats[:, h, bass.ds(j, 1), :].rearrange("p a n -> p (a n)"), xs).then_inc(x2_stat, 1)

                def body(before, parity, first, last):
                    j = before + (0 if first else 1)
                    pairs = dve.compute_val(b * BLOCKS * PAIRS + j * PAIRS)
                    maxes = dve.compute_val(b * BLOCKS * MAXES + j * MAXES + MAXES)
                    nxt = dve.compute_val(b * BLOCKS + j + 1)
                    col = dve.compute_val(before * N)
                    free = own_banks(1 - parity)
                    for p in range(PAIRS):
                        if p == 0 and not first:
                            denominators(before, free)
                        if p == 12 and not last:
                            rows_out(nxt, free)
                        if p + 1 < PAIRS or not last:
                            low(pairs, p + 1)
                        if not last:
                            for m in range(PER_STEP * p, min(PER_STEP * (p + 1), MAXES)):
                                reduce(maxes, m, free)
                            if p == 11:
                                split_max(nxt, maxes)
                        if not first and p in (13, 14):
                            add_half(before, col, p - 13, free + 1 - (p - 13))

                low(dve.compute_val(b * BLOCKS * PAIRS), 0)
                body(0, 0, True, False)
                with dve.Fori(0, (BLOCKS - 2) // 2) as jj:
                    body(dve.compute_val(jj * 2), 1, False, False)
                    body(dve.compute_val(jj * 2 + 1), 0, False, False)
                body(BLOCKS - 2, 1, False, True)
                denominators(BLOCKS - 1, own_banks(1))
                for h in range(2):
                    add_half(BLOCKS - 1, (BLOCKS - 1) * N, h, own_banks(0) + 1 - h)
                settle(dve)
                dve.wait_ge(x2_stat, b * 2 * BLOCKS + 2 * BLOCKS)
                groupnorm(b, 1)

                def gate(c, t, dst, slots, col, before, after):
                    bank = 2 * (c % 3)
                    dve.wait_ge(before, b * SLOTS + c + 1)
                    dve.scalar_tensor_tensor(dst[0:HR, c % slots, :, :], t[0:HR, c % 2, :, :],
                                             w_all[0:HR, c // CHUNKS // 2, col:col + 1], ps[0:HR, bank:bank + 2, :],
                                             ALU.mult, ALU.add).then_inc(after, 1)

                def result(u):
                    s = u % 2
                    dve.wait_ge(sig_ready, b * UNITS + u + 1)
                    if u >= 1:
                        dve.wait_ge(res_ready, b * UNITS + u)
                    dve.tensor_tensor(dif, sig[:, 1, :], sig[:, 0, :], ALU.subtract).then_inc(dif_ready, 1)
                    dve.wait_ge(dif_ready, b * UNITS + u + 1)
                    dve.scalar_tensor_tensor(dif, dif, -1.0, dif, ALU.mult, ALU.max).then_inc(size_ready, 1)
                    dve.wait_ge(size_ready, b * UNITS + u + 1)
                    dve.wait_ge(x2t_in[u % 3], b * THIRD_UNITS * CHUNKS + 16 * CHUNKS * (u // 3 + 1))
                    if u >= 2:
                        dve.wait_ge(stored[s], b * HALF_UNITS + 16 * (u // 2))
                    dve.scalar_tensor_tensor(res[:, s, :], dif, 1e-6, x2t[:, u % 3, :], ALU.max,
                                             ALU.add).then_inc(res_ready, 1)

                def side(u, d):
                    s = u % 2
                    if d == 0:
                        dve.wait_ge(x4_in[s], b * HALF_UNITS * 4 + 64 * (u // 2 + 1))
                        if u >= 2:
                            dve.wait_ge(h1_mm, b * SLOTS + CHUNKS * (u - 1))
                    ins = dve.tensor_scalar(t0[HR:P, s, d, :], x4[HR:P, s, :], 0.5, None,
                                            ALU.subtract if d == 0 else ALU.add)
                    if d == 1:
                        ins.then_inc(x_side, 1)

                side(0, 0)
                side(0, 1)
                dve.wait_ge(coef_step, COEF_STEPS)
                following = None if last else dve.compute_val(b + 1)
                for s in range(SLOTS + 1):
                    if s < SLOTS:
                        if s >= 2:
                            dve.wait_ge(h2_mm, b * SLOTS + s - 1)
                        gate(s, t1, h1, 2, SC_T1, t1_ready, h1_ready)
                    if 1 <= s <= SLOTS:
                        if s > H2_SLOTS:
                            dve.wait_ge(h3_mm, b * UNITS + (s - 1 - H2_SLOTS) // CHUNKS + 1)
                        gate(s - 1, t2, h2, H2_SLOTS, SC_T2, t2_ready, h2_ready)
                    if s % CHUNKS in (1, 2) and s // CHUNKS + 1 < UNITS:
                        side(s // CHUNKS + 1, s % CHUNKS - 1)
                    if s >= 8 and (s - 8) % CHUNKS == 0 and (s - 8) // CHUNKS < UNITS - 2:
                        result((s - 8) // CHUNKS)
                    if not last and STATS_AT <= s < STATS_AT + BLOCKS:
                        statistics(following, 0, s - STATS_AT)
                    if not last and SLOTS - 3 <= s < SLOTS:
                        for j in range(2):
                            statistics(following, 1, 2 * (s - SLOTS + 3) + j)
                result(UNITS - 2)
                if not last:
                    for j in range(6, BLOCKS):
                        statistics(following, 1, j)
                    first_norm(following)
                result(UNITS - 1)

            for j in range(BLOCKS):
                statistics(0, 1, j)
            first_norm(0)
            with dve.Fori(0, B - 1) as b:
                image(b, False)
            image(B - 1, True)

        @block.tensor
        def _(pe):
            pe.wait_ge(consts_in, CONST_DMAS * 16)
            pe.wait_ge(set_gp, 1)
            pe.wait_ge(set_step, SETUP_STEPS)

            def averages(b, k):
                pe.wait_ge(stat_step, b * 2 * STAT_STEPS + k * STAT_STEPS + 1)
                pe.matmul(ps[0:HALF, 0, 0:2], g6_sb[:, :], mv[:, :, 0], start=True, stop=True
                          ).then_inc(stat_mm, 1)
                pe.wait_ge(stat_step, b * 2 * STAT_STEPS + k * STAT_STEPS + 5)
                pe.matmul(ps[0:HALF, 1, 0:2], g6_sb[:, :], tmp_a[:, :], start=True, stop=True
                          ).then_inc(stat_mm, 1)

            def image(b, last):
                def bank_free(n):
                    if n >= 4:
                        pe.wait_ge(proj_act, b * BANKS + n - 3)

                for n in range(QK_BANKS):
                    bank_free(n)
                    if n % 2 == 0:
                        pe.wait_ge(xn_ready, b * (FIRST_PIECES + SECOND_PIECES) + n + 2)
                    for h in range(2):
                        ins = pe.matmul(ps[:, n % 4, :], wqk_sb[:, h, :], xn[0:HALF, h, n * N:(n + 1) * N],
                                        start=(h == 0), stop=(h == 1))
                    ins.then_inc(proj_mm, 1)

                def max_tile(base, q_col, m, bank, evacuated):
                    if m >= 2:
                        pe.wait_ge(max_red, base + m - 1)
                    elif evacuated is not None:
                        pe.wait_ge(out_norm, evacuated + START)
                    pe.matmul(ps[:, bank + m % 2, :], qst[:, bass.ds(q_col + (m // BLOCKS) * P, P)],
                              kst[:, (m % BLOCKS) * N:(m % BLOCKS + 1) * N], start=True, stop=True
                              ).then_inc(max_mm, 1)

                def turn_max(g, bank):
                    pe.wait_ge(max_step, g * MAX_STEPS + MAX_STEPS)
                    pe.transpose(ps[0:3 * NT, bank, 0:P // 2].bitcast(F16), mparts[:, :, :]
                                 .rearrange("p r t -> p (r t)"), eye16[:, :]).then_inc(max_turn, 1)

                maxes0 = pe.compute_val(b * BLOCKS * MAXES)
                blocks0 = pe.compute_val(b * BLOCKS)

                def value_bank(v):
                    n = QK_BANKS + v
                    bank_free(n)
                    for k in range(2):
                        m = 2 * v + k
                        pe.matmul(ps[:, n % 4, k * C:(k + 1) * C], xn[0:HALF, 0, m * P:(m + 1) * P],
                                  wv_sb[0:HALF, 0, :], start=True, stop=False)
                        ins = pe.matmul(ps[:, n % 4, k * C:(k + 1) * C], xn[:, 1, m * P:(m + 1) * P],
                                        wv_sb[:, 1, :], start=False, stop=True)
                    ins.then_inc(proj_mm, 1)

                value_bank(0)
                value_bank(1)
                for v in range(V_BANKS):
                    if v + 2 < V_BANKS:
                        value_bank(v + 2)
                    if v == FIRST_SPLIT + 1:
                        turn_max(blocks0, own_banks(0))
                    for m in first_maxes(v):
                        if m < BLOCKS and m % 2 == 0:
                            pe.wait_ge(stacks_in[m // 2], b * (STACK_DMAS * 16) + STACK_DMAS * 16)
                        if m >= 4 and m % 2 == 0:
                            pe.wait_ge(max_red, maxes0 + m - 2)
                        pe.matmul(ps[:, 4 + m % 4, :], qst[:, m // BLOCKS * P:(m // BLOCKS + 1) * P],
                                  kst[:, (m % BLOCKS) * N:(m % BLOCKS + 1) * N], start=True, stop=True
                                  ).then_inc(max_mm, 1)

                def turn_out(slot, h, bank):
                    for t in range(NT):
                        ins = pe.transpose(ps[0:HALF, bank, t * P:(t + 1) * P],
                                           o_sb[:, slot, t, h * HALF:(h + 1) * HALF], eye_sb[:, :])
                    ins.then_inc(out_turn, 1)

                def scores(pairs, q_col, q):
                    for i in range(2):
                        m = (2 * q + i) % MT
                        ins = pe.matmul(ps[:, 2 * (q % 2) + i, :], kst[:, m * P:(m + 1) * P],
                                        qst[:, bass.ds(q_col, N)], start=True, stop=True)
                    ins.then_inc(scored, 1)

                def body(before, parity, first, last):
                    j = before + (0 if first else 1)
                    pairs = pe.compute_val(b * BLOCKS * PAIRS + j * PAIRS)
                    maxes = pe.compute_val(b * BLOCKS * MAXES + j * MAXES + MAXES)
                    blocks = pe.compute_val(b * BLOCKS + j)
                    q_col = pe.compute_val(j * N)
                    q_next = pe.compute_val(j * N + N)
                    mine, free = own_banks(parity), own_banks(1 - parity)
                    for p in range(PAIRS):
                        if p == 12 and not last:
                            turn_max(blocks + 1, free)
                        if p + 2 < PAIRS or not last:
                            pe.wait_ge(full_ready, pairs + p + 1)
                            if p + 2 == PAIRS:
                                pe.wait_ge(max_in, blocks * 16 + 32)
                            scores(pairs, q_col if p + 2 < PAIRS else q_next, p + 2)
                        pe.wait_ge(lo_ready, pairs + p + 1)
                        if p == 0 and first:
                            pe.wait_ge(v_done, b * V_BANKS + V_BANKS)
                            pe.wait_ge(ones_col, b + 1)
                        if p == 0 and not first:
                            pe.wait_ge(x2_ready, b * 2 * BLOCKS + 2 * before + START)
                        todo = list(range(PER_STEP * p, min(PER_STEP * (p + 1), MAXES))) if not last else []
                        spots = (5, 6, 7) if p == 0 else (2, 5, 7)
                        for i in range(2):
                            m = 2 * p + i
                            for t in range(NT):
                                eh = e_hi[:, p % 4, i * N + t * P:i * N + (t + 1) * P]
                                el = e_lo[:, p % 4, i * N + t * P:i * N + (t + 1) * P]
                                acc = ps[:, mine + t // 2, (t % 2) * 256:(t % 2) * 256 + C + 1]
                                pe.matmul(acc, eh, v_sb[:, m, 0:C + 1], start=(m == 0 and t % 2 == 0), stop=False,
                                          skip_group_check=True)
                                pe.matmul(acc[:, 0:C], eh, v_sb[:, m, VW:VW + C], start=False, stop=False,
                                          skip_group_check=True)
                                ins = pe.matmul(acc, el, v_sb[:, m, 0:C + 1], start=False, stop=(m == MT - 1),
                                                skip_group_check=True)
                                if i == 1 and t == NT - 1:
                                    ins.then_inc(summed, 1)
                                if i * NT + t in spots and todo:
                                    max_tile(maxes, q_next, todo.pop(0), free,
                                             None if first else blocks)
                        if not first and p in (12, 13):
                            if p == 12:
                                pe.wait_ge(out_norm, blocks + START)
                            elif not last:
                                pe.wait_ge(max_rows, blocks + 2)
                            turn_out(1 - parity, p - 12, free + 1 - (p - 12))

                pe.wait_ge(max_in, b * BLOCKS * 16 + 16)
                pe.wait_ge(proj_act, b * BANKS + BANKS)
                pairs0 = pe.compute_val(b * BLOCKS * PAIRS)
                scores(pairs0, 0, 0)
                scores(pairs0, 0, 1)
                body(0, 0, True, False)
                with pe.Fori(0, (BLOCKS - 2) // 2) as jj:
                    body(pe.compute_val(jj * 2), 1, False, False)
                    body(pe.compute_val(jj * 2 + 1), 0, False, False)
                body(BLOCKS - 2, 1, False, True)
                pe.wait_ge(out_norm, b * BLOCKS + BLOCKS + START)
                pe.wait_ge(x2_ready, b * 2 * BLOCKS + 2 * BLOCKS - 2 + START)
                for h in range(2):
                    turn_out(1, h, own_banks(0) + 1 - h)
                averages(b, 1)

                pe.wait_ge(set_gp, 2)
                for s in range(SLOTS + 2):
                    if s < SLOTS:
                        u, k = s // CHUNKS, s % CHUNKS
                        if k % 2 == 0:
                            pe.wait_ge(t0_ready, b * SLOTS + s + 2)
                        if k == 0:
                            pe.wait_ge(x_side, b * UNITS + u + 1)
                        if s >= 3:
                            pe.wait_ge(h2_ready, b * SLOTS + s - 2)
                        for d in range(2):
                            ins = pe.matmul(ps[0:HR, 2 * (s % 3) + d, :], w_all[:, u // 2, 0:HR],
                                            t0[:, u % 2, d, k * N:(k + 1) * N], start=True, stop=True)
                        ins.then_inc(h1_mm, 1)
                    if 1 <= s <= SLOTS:
                        c = s - 1
                        pe.wait_ge(h1_ready, b * SLOTS + c + 1)
                        for d in range(2):
                            ins = pe.matmul(ps[0:HR, 2 * (c % 3) + d, :], w_all[0:HR, c // CHUNKS // 2, HR:2 * HR],
                                            h1[0:HR, c % 2, d, :], start=True, stop=True)
                        ins.then_inc(h2_mm, 1)
                    if s >= CHUNKS + 1 and (s - 1) % CHUNKS == 0:
                        u = (s - 1) // CHUNKS - 1
                        pe.wait_ge(h2_ready, b * SLOTS + CHUNKS * (u + 1))
                        if u >= 1:
                            pe.wait_ge(lu_ready, b * UNITS + u)
                        for d in range(2):
                            for k in range(CHUNKS):
                                ins = pe.matmul(ps[k * G:(k + 1) * G, 6 + d, :],
                                                w_all[0:HR, u // 2, 2 * HR:WCOLS],
                                                h2[0:HR, (CHUNKS * u + k) % H2_SLOTS, d, :], start=True, stop=True)
                        ins.then_inc(h3_mm, 1)

                if not last:
                    averages(pe.compute_val(b + 1), 0)

            averages(0, 0)
            with pe.Fori(0, B - 1) as b:
                image(b, False)
            image(B - 1, True)


def layout(inputs):
    import numpy as np
    a = {k: np.asarray(v) for k, v in inputs.items()}
    f = np.float32
    wqk = np.zeros((C, P), f)
    cols = np.zeros((P, NCOLS), f)
    for k, which in enumerate((2, 2, 1, 1)):
        wqk[:, k * SUB:k * SUB + CR] = a[f"L0_conv_w{which}"].T
        cols[k * SUB:k * SUB + CR, COL_B] = a[f"L0_conv_b{which}"]
        cols[k * SUB:(k + 1) * SUB, COL_A] = a[f"L0_conv_a{which}"]
    cols[CR:CR + 3, COL_B] = (BIG, 1.0, 1.0)
    cols[:, COL_AA] = a["L0_conv_aa"]
    cols[SUB:2 * SUB, COL_M] = cols[3 * SUB:, COL_M] = -1.0
    wv = np.concatenate([a["L0_conv_wa"].T, a["L0_conv_ba"][None, :]], 0)
    per = C // 32
    g6 = np.kron(np.eye(HALF // per, dtype=f), np.full((per, per), 1.0 / per, f))
    diag = np.tile(np.eye(G, dtype=f), (4, 1))

    def rows(of):
        parts = [of(min(j, HID - 1)).reshape(GROUPS, G, -1).transpose(1, 0, 2) for j in range(4)]
        return np.ascontiguousarray(np.concatenate(parts, 0))

    m0, m1, m2, m3 = (a[f"L1_conv_m{i}"] for i in range(4))
    b0, b1, b2, b3 = (a[f"L1_conv_b{i}"][:, :, 0] for i in range(4))
    f0, f1, f2 = (a[f"L1_conv_f{i}"][:, :, 0] for i in range(3))
    mraw = rows(lambda j: np.concatenate([
        m0[:, :, 0], m1.reshape(C, 9), m2.reshape(C, 9), m3[:, 0, :],
        m1[:, :, j], m2[:, :, j], m3[:, 0, j:j + 1], m0[:, j], m1[:, j, :], m2[:, j, :]], 1))
    fraw = rows(lambda j: np.stack([f0[:, j], f1[:, j], f2[:, j]], 1))
    braw = rows(lambda j: np.concatenate([b0, b1, b2, b3, b0[:, j:j + 1], b1[:, j:j + 1], b2[:, j:j + 1]], 1))
    return {"x": np.ascontiguousarray(a["x"]), "wqk": wqk, "wv": np.ascontiguousarray(wv), "cols": cols, "g6": g6,
            "eye": np.eye(P, dtype=f), "diag": diag, "mraw": mraw, "fraw": fraw, "braw": braw}


def kernel(**inputs):
    import concourse.bacc as bacc
    from concourse.bass_utils import run_bass_kernel_spmd

    nc = bacc.Bacc("TRN2", target_bir_lowering=False, num_devices=1)
    arrays = layout(inputs)
    args = [nc.dram_tensor(f"{name}_dram", a.shape, mybir.dt.from_np(a.dtype), kind="ExternalInput").ap()
            for name, a in arrays.items()]
    out = nc.dram_tensor("out_dram", arrays["x"].shape, F32, kind="ExternalOutput").ap()
    program(nc, *args, out)
    r = run_bass_kernel_spmd(nc, [{f"{name}_dram": a for name, a in arrays.items()}], core_ids=[0])
    return r.results[0]["out_dram"]
```
